# Optimizing a Trainium2 kernel written in Bass

```python
import numpy as np
import jax
import jax.numpy as jnp

def _softmax(x, axis=-1):
    return jax.nn.softmax(x, axis=axis)

def _gelu(x):
    return jax.nn.gelu(x, approximate=True)

def _silu(x):
    return jax.nn.silu(x)

def _sigmoid(x):
    return jax.nn.sigmoid(x)

def _layernorm(x, axis=-1, eps=1e-05):
    m = jnp.mean(x, axis=axis, keepdims=True)
    v = jnp.var(x, axis=axis, keepdims=True)
    return (x - m) / jnp.sqrt(v + eps)

def _scatter_add(tgt, idx, src, axis=0):
    return tgt.at[idx].add(src)

def _segment_sum(src, seg, n):
    return jax.ops.segment_sum(src, seg, n)
kernel_name = 'mk_audio_tower_d1_tok_audfeat256_r4_3b5fea'

def setup_inputs(seed: int=0):
    np.random.seed(seed)
    _w = jnp.asarray

    def _rec_inputs():
        import jax
        import jax.numpy as jnp
        _rk = jax.random.key(seed)
        x = -0.000392918 + 0.999932 * jax.random.normal(jax.random.fold_in(_rk, 1), (4, 750, 128), jnp.float32)
        return x
    x = _rec_inputs()

    def _L0_tok_setup():
        import jax, jax.numpy as jnp
        from jax import lax
        import numpy as np
        BN_EPS = 0.001

        @jax.custom_vjp
        def ste_sign(x):
            return jnp.where(x >= 0, 1.0, -1.0).astype(x.dtype)

        def _ste_fwd(x):
            return (ste_sign(x), x)

        def _ste_bwd(x, g):
            return (g * (jnp.abs(x) <= 1.0).astype(g.dtype),)
        ste_sign.defvjp(_ste_fwd, _ste_bwd)
        key = jax.random.key(seed)
        ks = jax.random.split(key, 6)
        x = jax.random.normal(ks[0], (64, 512, 128), dtype=jnp.float32)
        kernel = jax.random.normal(ks[1], (3, 128, 64), dtype=jnp.float32) * 0.05
        bias = jax.random.normal(ks[2], (64,), dtype=jnp.float32) * 0.01
        beta = jax.random.normal(ks[3], (64,), dtype=jnp.float32) * 0.01
        moving_mean = jax.random.normal(ks[4], (64,), dtype=jnp.float32) * 0.1
        moving_var = jax.random.uniform(ks[5], (64,), dtype=jnp.float32) + 0.5
        return {'x': x, 'kernel': kernel, 'bias': bias, 'beta': beta, 'moving_mean': moving_mean, 'moving_var': moving_var}
    _L0_tok_all = _L0_tok_setup()
    _L0_tok_in = {k: v for k, v in _L0_tok_all.items() if k in ('kernel', 'bias', 'beta', 'moving_mean', 'moving_var')}
    del _L0_tok_all

    def _L0_attn_setup():
        import jax, jax.numpy as jnp
        import numpy as np
        B, N, D, H = (4, 256, 64, 8)
        key = jax.random.key(seed)
        k1, k2, k3 = jax.random.split(key, 3)
        x = jax.random.normal(k1, (B, N, D), dtype=jnp.float32)
        Wqkv = jax.random.normal(k2, (D, 3 * D * H), dtype=jnp.float32) * 0.02
        bqkv = jnp.zeros((3 * D * H,), dtype=jnp.float32)
        W0 = jax.random.normal(k3, (D * H, D), dtype=jnp.float32) * 0.02
        b0 = jnp.zeros((D,), dtype=jnp.float32)
        return {'x': x, 'Wqkv': Wqkv, 'bqkv': bqkv, 'W0': W0, 'b0': b0}
    _L0_attn_all = _L0_attn_setup()
    _L0_attn_in = {k: v for k, v in _L0_attn_all.items() if k in ('Wqkv', 'bqkv', 'W0', 'b0')}
    del _L0_attn_all

    def _L0_ffn_setup():
        import jax, jax.numpy as jnp
        import numpy as np
        INPUT_WIDTH = 64
        DEPTH = 7
        OUTPUT_WIDTH = 64
        N_NODES = 2 ** (DEPTH + 1) - 1
        key = jax.random.key(seed)
        k_x, k_w1, k_w2 = jax.random.split(key, 3)
        init1 = 1.0 / np.sqrt(INPUT_WIDTH)
        x = jax.random.normal(k_x, (2, 256, INPUT_WIDTH), dtype=jnp.float32)
        w1s = jax.random.uniform(k_w1, (N_NODES, INPUT_WIDTH), jnp.float32, -init1, init1)
        b1s = jnp.zeros((N_NODES,), jnp.float32)
        w2s = jax.random.uniform(k_w2, (N_NODES, INPUT_WIDTH, OUTPUT_WIDTH), jnp.float32, -init1, init1)
        b2s = jnp.zeros((N_NODES, OUTPUT_WIDTH), jnp.float32)
        return {'x': x, 'w1s': w1s, 'b1s': b1s, 'w2s': w2s, 'b2s': b2s}
    _L0_ffn_all = _L0_ffn_setup()
    _L0_ffn_in = {k: v for k, v in _L0_ffn_all.items() if k in ('w1s', 'b1s', 'w2s', 'b2s')}
    del _L0_ffn_all
    return {'x': x, 'L0_tok_kernel': _L0_tok_in['kernel'], 'L0_tok_bias': _L0_tok_in['bias'], 'L0_tok_beta': _L0_tok_in['beta'], 'L0_tok_moving_mean': _L0_tok_in['moving_mean'], 'L0_tok_moving_var': _L0_tok_in['moving_var'], 'L0_attn_Wqkv': _L0_attn_in['Wqkv'], 'L0_attn_bqkv': _L0_attn_in['bqkv'], 'L0_attn_W0': _L0_attn_in['W0'], 'L0_attn_b0': _L0_attn_in['b0'], 'L0_ffn_w1s': _L0_ffn_in['w1s'], 'L0_ffn_b1s': _L0_ffn_in['b1s'], 'L0_ffn_w2s': _L0_ffn_in['w2s'], 'L0_ffn_b2s': _L0_ffn_in['b2s']}

def reference(x, L0_tok_kernel, L0_tok_bias, L0_tok_beta, L0_tok_moving_mean, L0_tok_moving_var, L0_attn_Wqkv, L0_attn_bqkv, L0_attn_W0, L0_attn_b0, L0_ffn_w1s, L0_ffn_b1s, L0_ffn_w2s, L0_ffn_b2s):
    import jax
    import jax.numpy as jnp

    def _L0_tok_ref(x, kernel, bias, beta, moving_mean, moving_var):
        import jax, jax.numpy as jnp
        from jax import lax
        import numpy as np
        BN_EPS = 0.001

        @jax.custom_vjp
        def ste_sign(x):
            return jnp.where(x >= 0, 1.0, -1.0).astype(x.dtype)

        def _ste_fwd(x):
            return (ste_sign(x), x)

        def _ste_bwd(x, g):
            return (g * (jnp.abs(x) <= 1.0).astype(g.dtype),)
        ste_sign.defvjp(_ste_fwd, _ste_bwd)
        xq = ste_sign(x)
        kq = ste_sign(kernel)
        y = lax.conv_general_dilated(xq, kq, window_strides=(1,), padding='VALID', dimension_numbers=('NWC', 'WIO', 'NWC'))
        y = y + bias
        inv = lax.rsqrt(moving_var + BN_EPS)
        return (y - moving_mean) * inv + beta

    def _L0_attn_ref(x, Wqkv, bqkv, W0, b0):
        import jax, jax.numpy as jnp
        import numpy as np
        B, N, D, H = (4, 256, 64, 8)
        b, n, d = x.shape
        h = Wqkv.shape[1] // (3 * d)
        qkv = x @ Wqkv + bqkv
        q, k, v = jnp.reshape(qkv, (3, b, n, d, h))
        score = jnp.einsum('bnqh,btqh->bnth', q, k) * d ** (-0.5)
        attn = jax.nn.softmax(score, axis=1)
        av = jnp.einsum('bnnh,bnqh->bnqh', attn, v)
        out = av.reshape(b, n, d * h) @ W0 + b0
        return out

    def _L0_ffn_ref(x, w1s, b1s, w2s, b2s):
        import jax, jax.numpy as jnp
        import numpy as np
        INPUT_WIDTH = 64
        DEPTH = 7
        OUTPUT_WIDTH = 64
        N_NODES = 2 ** (DEPTH + 1) - 1
        B, S, D = x.shape
        flat_x = x.reshape(B * S, D)
        T = flat_x.shape[0]
        current = jnp.zeros((T,), dtype=jnp.int32)
        all_nodes = []
        all_logits = []
        for _ in range(DEPTH + 1):
            all_nodes.append(current)
            score = jnp.einsum('td,td->t', flat_x, w1s[current]) + b1s[current]
            all_logits.append(score)
            choice = ((jnp.sign(score) + 1.0) / 2.0).astype(jnp.int32)
            current = current * 2 + choice + 1
        logits = jnp.stack(all_logits, axis=1)
        path_weights = jax.nn.gelu(jnp.abs(logits), approximate=False)
        out = jnp.zeros((T, OUTPUT_WIDTH), dtype=x.dtype)
        for i in range(DEPTH + 1):
            nodes_i = all_nodes[i]
            t_i = jnp.einsum('td,tdo->to', flat_x, w2s[nodes_i]) + b2s[nodes_i]
            out = out + t_i * path_weights[:, i][:, None]
        return out.reshape(B, S, OUTPUT_WIDTH)
    h = _L0_tok_ref(x, L0_tok_kernel, L0_tok_bias, L0_tok_beta, L0_tok_moving_mean, L0_tok_moving_var)
    h = h + _L0_attn_ref(_layernorm(h, axis=-1), L0_attn_Wqkv, L0_attn_bqkv, L0_attn_W0, L0_attn_b0)
    h = h + _L0_ffn_ref(_layernorm(h, axis=-1), L0_ffn_w1s, L0_ffn_b1s, L0_ffn_w2s, L0_ffn_b2s)
    return h

_drawn_inputs = setup_inputs


def setup_inputs(seed=0):
    import zlib

    import numpy as np

    out = dict(_drawn_inputs(seed))
    spreads = {'L0_attn_bqkv': (0.0, 2.0),
     'L0_attn_b0': (0.0, 0.8),
     'L0_ffn_b1s': (0.0, 0.367),
     'L0_ffn_b2s': (0.0, 0.8)}
    factors = {'L0_tok_bias': 57.177,
     'L0_tok_beta': 50.571,
     'L0_tok_moving_mean': 8.0,
     'L0_attn_Wqkv': 64.0,
     'L0_attn_W0': 64.0}
    for name, (base, spread) in spreads.items():
        noise = np.random.default_rng([zlib.crc32(name.encode()), seed]).standard_normal(out[name].shape)
        drawn = base * np.exp(spread * noise) if base else spread * noise
        out[name] = jnp.asarray(drawn.astype(out[name].dtype))
    for name, factor in factors.items():
        out[name] = (out[name] * factor).astype(out[name].dtype)
    return out
```

```python
from contextlib import ExitStack

import numpy as np
import concourse.bass as bass
from concourse import mybir

B, NIN, CIN = 4, 750, 128
TAPS, D = 3, 64
N = NIN - TAPS + 1
H = 8
NPAIR = H // 2
DEPTH = 8
NODES = 2 ** DEPTH - 1
LEAVES = 2 ** (DEPTH - 1)
P = 128
NT = -(-N // P)
START = [min(t * P, N - P) for t in range(NT)]
DUP = NT * P - N
TT = B * NT
XP = 125
XB = NIN // XP
T = B * N
NP3 = 250
QN = 3 * NP3
PAD = QN + 2
XW = T + 2
G = 32
OVG = 96
STAT = LEAVES * G
SLOTS = STAT + OVG * G
ST_TILES, OV_TILES = STAT // P, OVG * G // P
F_TILES = ST_TILES + OV_TILES
C_ONE, C_W, C_H, C_ID = D, D + 1, D + 1 + DEPTH, 2 * D + 1 + DEPTH
RW = C_ID + 1
BIG = 1 << 20
LN_EPS, BN_EPS = 1e-5, 1e-3
PT = [0, 128, 160, 168]
PENT = 170
OVCOL = 3


def tower(nc, x, k_tok, bias, beta, mean, var, Wqkv, bqkv, W0, b0, w1s, b1s, w2s, b2s, rows, out, dbg):
    f32, f16, bf16, i32, u32 = (mybir.dt.float32, mybir.dt.float16, mybir.dt.bfloat16,
                                mybir.dt.int32, mybir.dt.uint32)
    ALU = mybir.AluOpType
    ACT = mybir.ActivationFunctionType
    X = mybir.AxisListType.X
    ctx = ExitStack()
    with ctx:
        def sb(name, shape, dt=f32):
            return ctx.enter_context(nc.sbuf_tensor(name, shape, dt))

        def sem(name):
            return ctx.enter_context(nc.semaphore(name))

        wtab = sb("wtab", [P, PENT * D])
        pool_a = sb("pool_a", [P, 13 * PAD])
        st = pool_a[:, 0:6 * 3 * PAD // 2].bitcast(f16).rearrange("p (r a h n) -> p r a h n", r=3, a=3, h=2)
        qst, kst = st[:, :, 0], st[:, :, 1:3]
        hl0 = 6 * 3 * PAD // 2
        hl = pool_a[:, hl0:hl0 + 4 * PAD].bitcast(f16).rearrange("p (r k s n) -> p r k s n", r=2, k=2, s=2)
        btab = pool_a[0:32, 0:(LEAVES + OVCOL) * D]
        xhT = sb("xhT", [P, XW], f16)
        wq = sb("wq", [P, 2, 3 * H * D], f16)
        q32 = sb("q32", [P, 2, PAD])
        k32 = sb("k32", [P, 2, PAD])
        qk = sb("qk", [P, NT * P])
        vT = sb("vT", [P, 8, PAD])
        avT = sb("avT", [P, NPAIR, NT * P])
        xrow = sb("xrow", [P, TT, RW])
        xT2 = sb("xT2", [D + 1, NT * P])
        lm = sb("lm", [P, 2, NT, 256])
        L, M = lm[:, 0], lm[:, 1]
        ML = sb("ML", [P, NT, 256])
        axp = ML[:].rearrange("p t n -> p (t n)").bitcast(f16).rearrange(
            "p (r a t h d) -> p r a t h d", r=2, a=2, t=NT, h=2)
        gt = sb("gt", [P, NT, LEAVES])
        m7 = sb("m7", [P, TT, LEAVES], bf16)
        run = sb("run", [P, NT + 1, LEAVES], bf16)
        xin = lm[0:XP].rearrange("p a t n -> p (a t n)")[:, 0:B * XB * CIN].rearrange(
            "p (j c) -> p j c", c=CIN)
        sgn = avT[0:XP].rearrange("p j n -> p (j n)")[:, 0:B * XB * CIN // 2].bitcast(bf16).rearrange(
            "p (j c) -> p j c", c=CIN)
        wst = vT[:].rearrange("p j n -> p (j n)")[:, 0:3 * H * D]
        xT = ML[:].rearrange("p t n -> p (t n)")[:, 0:NIN].bitcast(bf16).rearrange("p (r n) -> p r n", r=2)
        cent = sb("cent", [P, NT, D])
        sq = sb("sq", [P, NT, D])
        xhl = sb("xhl", [P, NT, 2, D], f16)
        kk = sb("kk", [P, TAPS, D])
        kq = sb("kq", [P, TAPS, D], bf16)
        par = sb("par", [P, 5, D])
        bnA = sb("bnA", [P, D])
        bnC = sb("bnC", [P, D])
        half = sb("half", [P, D])
        bqn = sb("bqn", [P, 3, H])
        bq = sb("bq", [P, 12])
        bq8 = sb("bq8", [P, 12])
        w0p = sb("w0p", [P, NPAIR, D])
        w1n = sb("w1n", [P, 2, D])
        w1T = sb("w1T", [D + 1, 256])
        idf = sb("idf", [P, P])
        idb = sb("idb", [P, P], bf16)
        idh = sb("idh", [P, P], f16)
        tri = sb("tri", [P, P], bf16)
        tri_i = sb("tri_i", [P, P], bf16)
        ones = sb("ones", [P, P], bf16)
        sel = sb("sel", [P, 2])
        gmask = sb("gmask", [P, 4])
        valid = sb("valid", [P, 1])
        nm = sb("nm", [P, 2, NPAIR, 2 * NT])
        sm = sb("sm", [P, 2, NPAIR, 2 * NT])
        dg = sb("dg", [P, 2, NPAIR, 2 * NT])
        at = sb("at", [P, 2, NPAIR, 2 * NT])
        ath = sb("ath", [P, 2, NPAIR, 2 * NT], f16)
        ln1 = sb("ln1", [P, 4, NT])
        ln2 = sb("ln2", [P, 4, NT])
        lg = sb("lg", [P, TT, DEPTH])
        rank = sb("rank", [P, TT])
        leaf = sb("leaf", [P, TT])
        sc = sb("sc", [P, 4, TT])
        slot = sb("slot", [P, TT], i32)
        pw2 = sb("pw2", [P, DEPTH - 1])
        ogi = sb("ogi", [P, 2], i32)
        og = sb("og", [P, 1], bf16)
        endg = sb("endg", [P, 1])
        ovb = sb("ovb", [P, LEAVES])
        giota = sb("giota", [P, OVG])
        ind = sb("ind", [P, OVG], bf16)
        lami = sb("lami", [1, 2, OVG], i32)
        goff = gt[0:1].rearrange("p t n -> p (t n)").bitcast(i32).rearrange("p (g c) -> p g c", c=8)
        gpos = sb("gpos", [1, OVG], i32)
        NX = 4
        xs = vT[:].rearrange("p j n -> p (j n)")[:, 0:NX * 4 * RW].rearrange("p (r t c) -> p r t c", r=NX, t=4)
        ZW = DEPTH * D + 32
        z0 = NX * 4 * RW
        z = vT[:].rearrange("p j n -> p (j n)")[:, z0:z0 + 2 * ZW].rearrange("p (r c) -> p r c", r=2)
        zT = avT[:].rearrange("p j n -> p (j n)")[:, 0:3 * 512].rearrange("p (r c) -> p r c", r=3)
        eT = avT[0:32].rearrange("p j n -> p (j n)")[:, 3 * 512:3 * 640].rearrange("p (r c) -> p r c", r=3)
        NO = 8
        yo = lm[:].rearrange("p a t n -> p (a t n)")[:, 0:NO * D].rearrange("p (r c) -> p r c", r=NO)
        ysd = lm[:].rearrange("p a t n -> p (a t n)")[:, NO * D:]

        S = [ctx.enter_context(nc.psum_tensor(f"S{i}", [P, 1024], f32)) for i in range(3)]
        U = ctx.enter_context(nc.psum_tensor("U", [P, 1024], f32))
        U_D = 1000

        (s_par, s_w, s_bq, s_w0, s_w1, s_b1, s_tab, s_btab, s_fill, s_id, s_seg) = [
            sem(n) for n in ("params_in", "wqkv_in", "bq_in", "w0_in", "w1_in",
                             "b1_in", "table_in", "btab_in", "rows_filled", "consts_ready", "scatter_done")]
        (s_sgn, s_xtp, s_xtc, s_cv, s_h, s_sum, s_rs, s_xn, s_hi, s_xhl, s_xhp, s_xhT, s_wq, s_bn, s_kq, s_w1p,
         s_w1c, s_hb) = [sem(n) for n in (
            "signs", "x_blocks_T", "x_blocks_copied", "conv_done", "h_ready", "ln_sums", "ln_rstd", "ln_x",
            "x_hi", "x_lo", "xhat_T", "xhat_copied", "wq_split", "bn_ready", "kq_ready", "w1_T", "w1_copied",
            "h_plus_b0")]
        (s_uf, s_ue, s_score, s_max, s_exp, s_qc, s_kc, s_lo, s_prod, s_av) = [sem(n) for n in (
            "unit_filled", "unit_emptied", "scores", "maxima", "exps", "qk_hi_q", "qk_hi_k", "qk_lo", "qk_prod",
            "av_ready")]
        s_xin = [sem(f"x_in{b}") for b in range(B)]
        s_xsr = [sem(f"rows_in{r}") for r in range(NX)]
        s_outr = [sem(f"out_written{r}") for r in range(NO)]
        s_st = [sem(f"stacks_in{r}") for r in range(3)]
        (s_ex1, s_ex2, s_at, s_h2, s_c2, s_ss2, s_xh2, s_ml, s_lg, s_m7, s_rk, s_gelu) = [sem(n) for n in (
            "diag_shifted", "diag_exp", "at_ready", "h2_ready", "ln2_squares", "ln2_sumsq", "xhat2_ready",
            "masked_logits", "path_logits", "leaf_masks", "ranks", "gelu_done")]
        (s_cnt, s_og, s_pre, s_ind, s_lam, s_goff, s_slot, s_abs, s_ovb) = [sem(n) for n in (
            "leaf_counts", "leaf_groups", "group_prefix", "group_index", "group_leaf", "group_offsets", "slots",
            "abs_logits", "ovb")]
        (s_z, s_zp, s_zc, s_y, s_yo) = [sem(n) for n in (
            "z_ready", "z_T", "zT_copied", "y_ready", "rows_out")]
        s_axp = sem("weights_expanded")
        s_bz = sem("btab_margins")
        vs, ps_, as_ = sem("vector_step"), sem("pool_step"), sem("scalar_step")

        def chain(engine, s):
            n = [0]

            def link(ins):
                n[0] += 1
                ins.then_inc(s, 1)
                engine.wait_ge(s, n[0])
            return link

        def extras(u):
            b, ph = u // NPAIR - 1, u % NPAIR
            if b < 0:
                return []
            return [[("bc", b, 0), ("bc", b, 1), ("bc", b, 2)], [("bc", b, 3), ("o", b, 0)],
                    [("t", b, 0), ("l", b, 0), ("l", b, 1)], [None, None, ("r", b, 0)]][ph]

        NU = B * NPAIR
        AHEAD = 2
        units = [(k, w, 0) for w in range(AHEAD) for k in "qkv"]
        for u in range(NU + NPAIR):
            if u < NU and u + AHEAD < NU:
                units += [(k, u + AHEAD, 0) for k in "qkv"]
            if u + AHEAD == NU:
                units.append(("d", NU - 1, 0))
            units += [e for e in extras(u) if e]
        unit_no = {k: n for n, k in enumerate(units)}

        def diag_unit(w):
            return unit_no[("v", w + 1, 0) if w + 1 < NU else ("d", w, 0)]

        block = ctx.enter_context(nc.Block())

        @block.sync
        def _(sp):
            xv = x.rearrange("b (j p) c -> p (b j) c", p=XP)
            for b in range(B):
                sp.dma_start(xin[:, b * XB:(b + 1) * XB, :], xv[:, b * XB:(b + 1) * XB, :]).then_inc(s_xin[b], 16)
                if b == 0:
                    sp.dma_start(kk[:], k_tok.rearrange("t c o -> c t o")).then_inc(s_par, 16)
                    for n, v in enumerate((bias, beta, mean, var, b0)):
                        sp.dma_start(par[:, n, :], v.partition_broadcast(P)).then_inc(s_par, 16)
            sp.dma_start(wst[0:D, :], Wqkv).then_inc(s_w, 16)
            sp.dma_start(wst[D:P, :], Wqkv).then_inc(s_w, 16)
            for a in range(2):
                sp.dma_start(bqn[a * D:(a + 1) * D], bqkv.rearrange("(g d h) -> d g h", g=3, d=D)).then_inc(s_bq, 16)
            w0v = W0.rearrange("(d j a) o -> a d j o", j=NPAIR, a=2)
            for a in range(2):
                sp.dma_start(w0p[a * D:(a + 1) * D, :, :], w0v[a]).then_inc(s_w0, 16)
            sp.dma_start(w1n[:, 0, :], w1s[0:P, :]).then_inc(s_w1, 16)
            sp.dma_start(w1n[0:NODES - P, 1, :], w1s[P:NODES, :]).then_inc(s_w1, 16)
            sp.dma_start(w1T[D:D + 1, 0:NODES], b1s.unsqueeze(0)).then_inc(s_b1, 16)
            sp.wait_ge(s_id, 1)
            sp.dma_start(rows.rearrange("(t p) c -> p t c", p=P),
                         xrow[:, 0:1, :].to_broadcast([P, F_TILES, RW])).then_inc(s_fill, 16)
            tv = wtab[:].rearrange("p (e o) -> p e o", o=D)
            wv = w2s.rearrange("n d o -> d n o")
            for i, lv in enumerate((6, 4, 2, 0)):
                n = 2 ** lv
                dst = tv[0:D, PT[i]:PT[i] + 2 * n, :].rearrange("p (e r) o -> p e r o", r=2)
                for r in range(2):
                    sp.dma_start(dst[:, :, r, :], wv[:, n - 1:2 * n - 1, :]).then_inc(s_tab, 16)
                sp.dma_start(tv[D:P, PT[i]:PT[i] + 2 * n, :], wv[:, 2 * n - 1:4 * n - 1, :]).then_inc(s_tab, 16)
            for w in range(NU):
                r, c = w % 3, w % 2
                sp.wait_ge(s_lo, 2 * w + 2)
                if w >= 3:
                    sp.wait_ge(s_score, 2 * NT * (w - 2))
                for a in range(2):
                    src = slice(a * D, (a + 1) * D)
                    for half_ in range(2):
                        dst = slice(half_ * D, (half_ + 1) * D)
                        sp.dma_start(qst[dst, r, a, 0:QN], hl[src, c, 0, half_, 0:QN]).then_inc(s_st[r], 16)
                        sp.dma_start(kst[dst, r, :, a, 0:QN], hl[src, c, 1, :, 0:QN]).then_inc(s_st[r], 16)
            sp.wait_ge(s_score, 2 * NT * NU)
            sp.wait_ge(s_bz, 1)
            bt = btab.rearrange("p (e o) -> p e o", o=D)
            for g in range(4):
                for lv in range(DEPTH):
                    n, rep = 2 ** lv, LEAVES // 2 ** lv
                    src = b2s[n - 1:2 * n - 1, :].rearrange("(a n) o -> a n o", a=1).unsqueeze(2)
                    dst = bt[g * 8 + lv:g * 8 + lv + 1, OVCOL - g:OVCOL - g + LEAVES, :].rearrange(
                        "p (n r) o -> p n r o", r=rep)
                    sp.dma_start(dst, src.to_broadcast([1, n, rep, D])).then_inc(s_btab, 16)
            rv = rows.rearrange("(t p) c -> p t c", p=P)
            sp.wait_ge(s_seg, 16 * TT)
            for k in range(F_TILES // 4):
                if k >= NX:
                    for t in range(4 * (k - NX), 4 * (k - NX) + 4):
                        sp.wait_ge(s_outr[t % NO], 16 * (t // NO + 1))
                sp.dma_start(xs[:, k % NX], rv[:, 4 * k:4 * k + 4, :]).then_inc(s_xsr[k % NX], 16)
            for r in range(NO):
                sp.wait_ge(s_outr[r], 16 * (F_TILES // NO))
            if dbg is not None:
                sp.dma_start(dbg, xrow[:].rearrange("p t c -> p (t c)")).then_inc(s_fill, 16)
                sp.wait_ge(s_fill, 32)

        @block.gpsimd
        def _(pool):
            gp = nc.gpsimd
            link = chain(pool, ps_)
            gp.memset(half[:], -0.5)
            gp.memset(ones[:], 1.0)
            gp.memset(xrow[:], 0.0)
            gp.memset(xhT[:, T:XW], 0.0)
            gp.memset(run[:, 0, :], 0.0)
            gp.memset(sel[:], 0.0)
            gp.memset(gmask[:], 1.0)
            gp.memset(valid[:], 1.0)
            gp.memset(idf[:], 0.0)
            link(gp.memset(tri[:], 1.0))
            link(gp.affine_select(out=idf[:], in_=idf[:], compare_op=ALU.not_equal, fill=1.0, base=0,
                                  pattern=[[-1, P]], channel_multiplier=1))
            link(gp.memset(sel[0:D, 0:1], 1.0))
            link(gp.memset(sel[D:P, 1:2], 1.0))
            gp.affine_select(out=valid[:], in_=valid[:], compare_op=ALU.is_ge, fill=0.0, base=-DUP,
                             pattern=[[0, 1]], channel_multiplier=1)
            link(gp.affine_select(out=gmask[:], in_=gmask[:], compare_op=ALU.is_ge, fill=0.0, base=0,
                                  pattern=[[-G, 4]], channel_multiplier=1))
            link(gp.affine_select(out=gmask[:], in_=gmask[:], compare_op=ALU.is_ge, fill=0.0, base=G - 1,
                                  pattern=[[G, 4]], channel_multiplier=-1))
            gp.tensor_copy(idb[:], idf[:])
            gp.tensor_copy(idh[:], idf[:])
            gp.affine_select(out=tri_i[:], in_=tri[:], compare_op=ALU.is_ge, fill=0.0, base=0,
                             pattern=[[1, P]], channel_multiplier=-1)
            link(gp.affine_select(out=tri[:], in_=tri[:], compare_op=ALU.is_gt, fill=0.0, base=0,
                                  pattern=[[1, P]], channel_multiplier=-1))
            gp.iota(giota[:], pattern=[[1, OVG]], base=0, channel_multiplier=0, allow_small_or_imprecise_dtypes=True)
            gp.iota(gpos[:], pattern=[[0, OVG // 4], [-1, 4]], base=OVCOL, channel_multiplier=0)
            for lv in range(DEPTH - 1):
                gp.memset(pw2[:, lv:lv + 1], float(2 ** (DEPTH - 2 - lv)))
            link(gp.memset(xrow[:, 0, C_ID:C_ID + 1].bitcast(i32), BIG))
            link(gp.memset(w1T[D:D + 1, NODES:256], 0.0))
            pool.sem_inc(s_id, 1)
            pool.wait_ge(s_par, 16 * 6)
            link(gp.tensor_scalar(bnA[:], par[:, 3, :], BN_EPS, 1.0, ALU.add, ALU.mult))
            link(gp.tensor_tensor(bnA[:], bnA[:], half[:], ALU.pow))
            link(gp.tensor_tensor(bnC[:], par[:, 0, :], par[:, 2, :], ALU.subtract))
            link(gp.tensor_tensor(bnC[:], bnC[:], bnA[:], ALU.mult))
            link(gp.tensor_tensor(bnC[:], bnC[:], par[:, 1, :], ALU.add))
            gp.tensor_scalar(bnA[:], bnA[:], 4.0, 0.0, ALU.mult, ALU.add).then_inc(s_bn, 1)
            pool.wait_ge(s_fill, 16)
            for t in range(TT):
                b, j = divmod(t, NT)
                gp.iota(xrow[:, t, C_ID:C_ID + 1].bitcast(i32), pattern=[[0, 1]], base=b * N + START[j],
                        channel_multiplier=1)
            link(gp.memset(xrow[:, :, C_ONE:C_ONE + 1], 1.0))

            for b in range(B):
                bt = slice(b * NT, (b + 1) * NT)
                pool.wait_ge(s_sum, b + 1)
                link(gp.tensor_scalar(ln1[:, 2, :], ln1[:, 1, :], 1.0 / D, LN_EPS, ALU.mult, ALU.add))
                gp.tensor_tensor(ln1[:, 3, :], ln1[:, 2, :], half[:, 0:NT], ALU.pow).then_inc(s_rs, 1)
                pool.wait_ge(s_hi, b + 1)
                gp.tensor_tensor(xhl[:, :, 1, :], sq[:], xhl[:, :, 0, :], ALU.subtract).then_inc(s_xhl, 1)
                gp.tensor_tensor(xrow[:, bt, C_H:C_ID], xrow[:, bt, C_H:C_ID],
                                 par[:, 4:5, :].to_broadcast([P, NT, D]), ALU.add).then_inc(s_hb, 1)

            def qk_lo(w):
                c = w % 2
                for n, (src, s_c) in enumerate(((q32, s_qc), (k32, s_kc))):
                    pool.wait_ge(s_c, w + 1)
                    gp.tensor_tensor(hl[:, c, n, 1, 0:QN], src[:, c, 0:QN], hl[:, c, n, 0, 0:QN],
                                     ALU.subtract).then_inc(s_lo, 1)
                if w >= 1:
                    pool.wait_ge(s_uf, diag_unit(w - 1) + 1)
                gp.tensor_tensor(qk[:, 0:N], q32[:, c, 0:N], k32[:, c, 0:N], ALU.mult).then_inc(s_prod, 1)

            def ln2_squares(b):
                pool.wait_ge(s_h2, b + 1)
                bt = slice(b * NT, (b + 1) * NT)
                link(gp.tensor_scalar(ln2[:, 2, :], ln2[:, 0, :], -1.0 / D, 0.0, ALU.mult, ALU.add))
                link(gp.tensor_tensor(cent[:], xrow[:, bt, C_H:C_ID],
                                      ln2[:, 2, :].unsqueeze(2).to_broadcast([P, NT, D]), ALU.add))
                gp.tensor_tensor(sq[:], cent[:], cent[:], ALU.mult).then_inc(s_c2, 1)

            def ln2_x(b):
                pool.wait_ge(s_ss2, b + 1)
                bt = slice(b * NT, (b + 1) * NT)
                link(gp.tensor_scalar(ln2[:, 2, :], ln2[:, 1, :], 1.0 / D, LN_EPS, ALU.mult, ALU.add))
                link(gp.tensor_tensor(ln2[:, 3, :], ln2[:, 2, :], half[:, 0:NT], ALU.pow))
                gp.tensor_tensor(xrow[:, bt, 0:D], cent[:],
                                 ln2[:, 3, :].unsqueeze(2).to_broadcast([P, NT, D]), ALU.mult).then_inc(s_xh2, 1)

            def routing(b):
                pool.wait_ge(s_ue, unit_no[("l", b, 1)] + 1)
                if b >= 1:
                    pool.wait_ge(s_lg, b)
                link(gp.memset(M[:, :, 0:1], 1.0))
                link(gp.tensor_scalar(gt[:, :, 0:LEAVES - 1], L[:, :, 0:LEAVES - 1], 0.0, None, ALU.is_gt))
                for lv in range(DEPTH - 1):
                    n = 2 ** lv
                    par_ = M[:, :, n - 1:2 * n - 1]
                    kid = M[:, :, 2 * n - 1:4 * n - 1].rearrange("p t (n c) -> p t n c", c=2)
                    link(gp.tensor_tensor(kid[:, :, :, 1], par_, gt[:, :, n - 1:2 * n - 1], ALU.mult))
                    link(gp.tensor_tensor(kid[:, :, :, 0], par_, kid[:, :, :, 1], ALU.subtract))
                gp.tensor_tensor(ML[:, :, 0:NODES], M[:, :, 0:NODES], L[:, :, 0:NODES], ALU.mult).then_inc(s_ml, 1)
                t0 = b * NT
                link(gp.tensor_copy(m7[:, t0:t0 + NT, :], M[:, :, LEAVES - 1:NODES]))
                link(gp.tensor_scalar(m7[:, t0 + NT - 1, :], m7[:, t0 + NT - 1, :], valid[:, 0:1], None, ALU.mult))
                if b >= 1:
                    pool.wait_ge(s_rk, b)
                    link(gp.tensor_copy(run[:, 0, :], run[:, NT, :]))
                for j in range(NT):
                    ins = gp.tensor_tensor(run[:, j + 1, :], run[:, j, :], m7[:, t0 + j, :], ALU.add)
                    link(ins)
                pool.sem_inc(s_m7, 1)

            def expand(b, j):
                if j == 0:
                    pool.wait_ge(s_at, b + 1)
                    if b >= 1:
                        pool.wait_ge(s_rk, b)
                if j >= 2:
                    pool.wait_ge(s_uf, unit_no[("bc", b, j - 2)] + 1)
                for a in range(2):
                    src = ath[:, a, j, :].rearrange("p (h t) -> p t h", h=2)
                    last = gp.tensor_copy(axp[:, j % 2, a], src.unsqueeze(3).to_broadcast([P, NT, 2, D]))
                last.then_inc(s_axp, 1)

            for w in range(AHEAD):
                qk_lo(w)
            for u in range(NU + NPAIR):
                b, ph = u // NPAIR - 1, u % NPAIR
                if u == NU:
                    pool.wait_ge(s_score, 2 * NT * NU)
                    gp.memset(btab[:, 0:OVCOL * D], 0.0)
                    gp.memset(btab[:, LEAVES * D:(LEAVES + OVCOL) * D], 0.0).then_inc(s_bz, 1)
                if b >= 0 and ph == 3:
                    routing(b)
                if b >= 0 and ph == 0:
                    expand(b, 0)
                    expand(b, 1)
                if b >= 0 and ph == 1:
                    expand(b, 3)
                if u + AHEAD < NU:
                    qk_lo(u + AHEAD)
                if b >= 0 and ph == 0:
                    expand(b, 2)
                if b >= 0 and ph == 1:
                    ln2_squares(b)
                    ln2_x(b)
            pool.wait_ge(s_slot, 1)
            pool.wait_ge(s_gelu, 1)
            for t in range(TT):
                gp.indirect_dma_start(rows, bass.IndirectOffsetOnAxis(slot[:, t:t + 1].bitcast(u32), 0),
                                      xrow[:, t, :], None, bounds_check=SLOTS - 1,
                                      oob_is_err=False).then_inc(s_seg, 16)
            outf = out.rearrange("b n o -> (b n) o")
            for k in range(F_TILES):
                pool.wait_ge(s_yo, k + 1)
                ids = xs[:, (k // 4) % NX, k % 4, C_ID:C_ID + 1]
                gp.indirect_dma_start(outf, bass.IndirectOffsetOnAxis(ids.bitcast(u32), 0), yo[:, k % NO, :], None,
                                      bounds_check=T - 1, oob_is_err=False).then_inc(s_outr[k % NO], 16)

        @block.tensor
        def _(pe):
            mm = nc.tensor.matmul
            pe.wait_ge(s_id, 1)
            pe.wait_ge(s_w1, 32)
            nc.tensor.transpose(U[0:D, 0:P], w1n[:, 0, :], idf[:])
            nc.tensor.transpose(U[0:D, P:NODES], w1n[0:NODES - P, 1, :],
                                idf[0:NODES - P, 0:NODES - P]).then_inc(s_w1p, 1)

            def x_blocks(b):
                pe.wait_ge(s_sgn, b + 1)
                if b >= 2:
                    pe.wait_ge(s_xtc, b - 1)
                xp = S[0][:, 512 * (b % 2):512 * (b % 2) + 384].bitcast(bf16).rearrange("p (j n) -> p j n", j=XB)
                for j in range(XB):
                    last = nc.tensor.transpose(xp[:, j, 0:XP], sgn[:, b * XB + j, :], idb[0:XP, 0:XP])
                last.then_inc(s_xtp, 1)

            def conv(b):
                pe.wait_ge(s_xtc, b + 1)
                pe.wait_ge(s_kq, 1)
                if b >= 2:
                    pe.wait_ge(s_h, b - 1)
                for j in range(NT):
                    o = 512 * (b % 2) + j * D
                    for k in range(TAPS):
                        last = mm(S[1][:, o:o + D], xT[:, b % 2, START[j] + k:START[j] + k + P], kq[:, k, :],
                                  start=(k == 0), stop=(k == TAPS - 1))
                last.then_inc(s_cv, 1)

            def xhat_T(b):
                pe.wait_ge(s_xhl, b + 1)
                if b >= 2:
                    pe.wait_ge(s_xhT, b - 1)
                xp = S[2][:, 512 * (b % 2):512 * (b % 2) + 384].bitcast(f16)
                for j in range(NT):
                    last = nc.tensor.transpose(xp[:, j * P:(j + 1) * P], xhl[:, j].rearrange("p a d -> p (a d)"),
                                               idh[:])
                last.then_inc(s_xhp, 1)

            x_blocks(0)
            x_blocks(1)
            for b in range(B):
                conv(b)
                if b + 2 < B:
                    x_blocks(b + 2)
                xhat_T(b)

            def fill(unit):
                if unit_no[unit]:
                    pe.wait_ge(s_ue, unit_no[unit])

            def project(kind, w):
                b, j = divmod(w, NPAIR)
                fill((kind, w, 0))
                base = "qkv".index(kind) * T + b * N
                for s in range(3):
                    r0, g = divmod(base + s, 3)
                    for a in range(2):
                        last = mm(U[:, 256 * s:256 * s + NP3], wq[:, a, g * H * D + j * P:g * H * D + (j + 1) * P],
                                  xhT[:, r0:r0 + NP3], start=(a == 0), stop=(a == 1))
                if kind == "v" and w >= 1:
                    last = diagonal(w - 1)
                last.then_inc(s_uf, 1)

            def diagonal(w):
                pe.wait_ge(s_prod, w + 1)
                for t in range(NT):
                    last = mm(U[:, U_D + t:U_D + t + NT + 1:NT], qk[:, START[t]:START[t] + P], sel[:],
                              start=True, stop=True)
                return last

            def broadcast(b, j):
                pe.wait_ge(s_axp, NPAIR * b + j + 1)
                fill(("bc", b, j))
                for t in range(NT):
                    for a in range(2):
                        last = mm(U[:, t * P:(t + 1) * P], axp[:, j % 2, a, t].rearrange("p h d -> p (h d)"),
                                  idh[:], start=(a == 0), stop=(a == 1))
                last.then_inc(s_uf, 1)

            def out_proj(b):
                if b == 0:
                    pe.wait_ge(s_w0, 32)
                pe.wait_ge(s_av, NPAIR * (b + 1))
                fill(("o", b, 0))
                for t in range(NT):
                    for j in range(NPAIR):
                        last = mm(U[:, t * D:(t + 1) * D], avT[:, j, t * P:(t + 1) * P], w0p[:, j, :],
                                  start=(j == 0), stop=(j == NPAIR - 1))
                last.then_inc(s_uf, 1)

            def x2_T(b):
                pe.wait_ge(s_xh2, b + 1)
                fill(("t", b, 0))
                for t in range(NT):
                    last = nc.tensor.transpose(U[0:D + 1, t * P:(t + 1) * P], xrow[:, b * NT + t, 0:D + 1], idf[:])
                last.then_inc(s_uf, 1)

            def logits(b, n):
                fill(("l", b, n))
                if n == 0:
                    pe.wait_ge(s_w1c, 1)
                    pe.wait_ge(s_b1, 16)
                for t in range(3):
                    last = mm(U[:, t * 256:(t + 1) * 256], xT2[:, (3 * n + t) * P:(3 * n + t + 1) * P], w1T[:],
                              start=True, stop=True)
                last.then_inc(s_uf, 1)

            def ranks(b):
                pe.wait_ge(s_m7, b + 1)
                fill(("r", b, 0))
                for t in range(NT):
                    mm(U[:, t * P:(t + 1) * P], tri[:], m7[:, b * NT + t, :], start=True, stop=False)
                    last = mm(U[:, t * P:(t + 1) * P], ones[:], run[:, t, :], start=False, stop=True)
                last.then_inc(s_uf, 1)

            def extra(u, n):
                es = extras(u)
                if n >= len(es) or es[n] is None:
                    return
                kind, b, k = es[n]
                if kind == "bc":
                    broadcast(b, k)
                elif kind == "o":
                    out_proj(b)
                elif kind == "t":
                    x2_T(b)
                elif kind == "l":
                    logits(b, k)
                else:
                    ranks(b)

            def scores(u, i):
                hd, t = divmod(i, NT)
                n = 2 * NT * u + i
                if i == 0:
                    pe.wait_ge(s_st[u % 3], 16 * 8 * (u // 3 + 1))
                if n >= 3:
                    pe.wait_ge(s_exp, n - 2)
                for a in range(2):
                    for c0, c1 in ((0, 512), (512, N)):
                        last = mm(S[n % 3][:, c0:c1], kst[:, u % 3, a, hd, START[t]:START[t] + P],
                                  qst[:, u % 3, hd, c0:c1], start=(a == 0), stop=(a == 1))
                last.then_inc(s_score, 1)

            pe.wait_ge(s_xhT, B)
            pe.wait_ge(s_wq, 1)
            pe.wait_ge(s_w1c, 1)
            for w in range(AHEAD):
                for kind in "qkv":
                    project(kind, w)
            for u in range(NU + NPAIR):
                for i in range(2 * NT):
                    if u < NU:
                        scores(u, i)
                    if i in (0, 2, 4) and u + AHEAD < NU:
                        project("qkv"[i // 2], u + AHEAD)
                    if i == 4 and u + AHEAD == NU:
                        fill(("d", NU - 1, 0))
                        diagonal(NU - 1).then_inc(s_uf, 1)
                    if i in (6, 8, 10):
                        extra(u, (i - 6) // 2)
            pe.wait_ge(s_m7, B)
            pe.wait_ge(s_ue, len(units))
            mm(U[:, 0:1], run[:, NT, :], ones[:, 0:1], start=True, stop=True).then_inc(s_cnt, 1)
            pe.wait_ge(s_og, 1)
            mm(U[:, 128:256], og[:].to_broadcast([P, P]), tri[:], start=True, stop=True)
            mm(U[:, 256:257], tri_i[:], og[:], start=True, stop=True).then_inc(s_pre, 1)
            pe.wait_ge(s_ind, 1)
            mm(U[0:1, 512:512 + OVG], ones[:, 0:1], ind[:], start=True, stop=True).then_inc(s_lam, 1)

            tv = wtab[:].rearrange("p (e o) -> p e o", o=D)
            pe.wait_ge(s_tab, 16 * 12)
            pe.wait_ge(s_btab, 16 * 32)

            def z_T(k):
                pe.wait_ge(s_z, k + 1)
                if k >= 2:
                    pe.wait_ge(s_zc, k - 1)
                zp = S[0][:, 512 * (k % 2):512 * (k % 2) + 512]
                ep = S[1][0:32, 512 * (k % 2):512 * (k % 2) + P]
                for i in range(4):
                    nc.tensor.transpose(zp[:, i * P:(i + 1) * P], z[:, k % 2, i * P:(i + 1) * P], idf[:])
                nc.tensor.transpose(ep, z[:, k % 2, 512:ZW], idf[:]).then_inc(s_zp, 1)

            z_T(0)
            for k in range(F_TILES):
                if k + 1 < F_TILES:
                    z_T(k + 1)
                pe.wait_ge(s_zc, k + 1)
                if k >= 2:
                    pe.wait_ge(s_yo, k - 1)
                if k < ST_TILES:
                    y = [S[2][:, 0:D], S[2][:, 512:512 + D]][k % 2]
                    for i, e in enumerate((PT[3] + k // 16, PT[2] + k // 4, PT[1] + k)):
                        mm(y, zT[:, k % 3, i * P:(i + 1) * P], tv[:, e, :], start=(i == 0), stop=False)
                    mm(y, eT[:, k % 3, :], btab[:, (4 * k + OVCOL) * D:(4 * k + OVCOL + 1) * D],
                       start=False, stop=False)
                    for g in range(4):
                        last = mm(y[g * G:(g + 1) * G, :], zT[:, k % 3, 3 * P + g * G:3 * P + (g + 1) * G],
                                  tv[:, 4 * k + g, :], start=False, stop=True)
                    last.then_inc(s_y, 1)
                else:
                    if k == ST_TILES:
                        pe.wait_ge(s_goff, 1)
                    y = [S[2][:, 0:4 * D], S[2][:, 512:512 + 4 * D]][k % 2]
                    for g in range(4):
                        q = 4 * (k - ST_TILES) + g
                        _, offs = nc.values_load_multi_w_load_instructions(
                            goff[0:1, q, 0:4], engines=(mybir.EngineType.PE,), min_val=0, max_val=(PENT - 1) * D)
                        _, boff = nc.values_load_multi_w_load_instructions(
                            goff[0:1, q, 4:5], engines=(mybir.EngineType.PE,), min_val=0,
                            max_val=(LEAVES + OVCOL - 1) * D)
                        for i in range(4):
                            mm(y[:, g * D:(g + 1) * D], zT[:, k % 3, i * P:(i + 1) * P],
                               wtab[:, bass.ds(offs[3 - i], D)], start=(i == 0), stop=False)
                        last = mm(y[:, g * D:(g + 1) * D], eT[:, k % 3, :],
                                  btab[:, bass.ds(boff[0], D)], start=False, stop=True)
                    last.then_inc(s_y, 1)

        @block.scalar
        def _(act):
            sc_ = nc.scalar
            act.wait_ge(s_w1p, 1)
            sc_.copy(w1T[0:D, 0:NODES], U[0:D, 0:NODES])
            act.wait_ge(s_id, 1)
            sc_.mul(w1T[0:D, NODES:256], idf[0:D, 0:1], 0.0).then_inc(s_w1c, 1)

            def x_copy(b):
                act.wait_ge(s_xtp, b + 1)
                if b >= 2:
                    act.wait_ge(s_cv, b - 1)
                xp = S[0][:, 512 * (b % 2):512 * (b % 2) + 384].bitcast(bf16).rearrange("p (j n) -> p j n", j=XB)
                sc_.copy(xT[:, b % 2, :].rearrange("p (j n) -> p j n", j=XB), xp[:, :, 0:XP]).then_inc(s_xtc, 1)

            x_copy(0)
            x_copy(1)
            for b in range(B):
                act.wait_ge(s_xn, b + 1)
                if b >= 1:
                    act.wait_ge(s_xhp, b)
                sc_.copy(xhl[:, :, 0, :], sq[:]).then_inc(s_hi, 1)
                if b + 2 < B:
                    x_copy(b + 2)
                act.wait_ge(s_xhp, b + 1)
                xp = S[2][:, 512 * (b % 2):512 * (b % 2) + 384].bitcast(f16)
                sc_.copy(xhT[:, b * N:b * N + START[-1]], xp[:, 0:START[-1]])
                sc_.copy(xhT[:, b * N + START[-1]:(b + 1) * N], xp[:, (NT - 1) * P:]).then_inc(s_xhT, 1)

            def diag_copy(w):
                b, j = divmod(w, NPAIR)
                if b >= 2 and j == 0:
                    act.wait_ge(s_ex1, b - 1)
                return sc_.copy(dg[:, b % 2, j, :], U[:, U_D:U_D + 2 * NT])

            def qkv_out(kind, w):
                b, j = divmod(w, NPAIR)
                if w == 0:
                    act.wait_ge(s_bn, 2)
                act.wait_ge(s_uf, unit_no[(kind, w, 0)] + 1)
                if kind != "v" and w >= 2:
                    act.wait_ge(s_prod, w - 1)
                if kind == "v" and w >= 8:
                    act.wait_ge(s_av, w - 7)
                dst = {"q": q32[:, w % 2, 0:QN], "k": k32[:, w % 2, 0:QN], "v": vT[:, w % 8, 0:QN]}[kind]
                base = "qkv".index(kind) * T + b * N
                for s in range(3):
                    g = (base + s) % 3
                    bv = (bq8 if kind == "q" else bq)[:, g * NPAIR + j:g * NPAIR + j + 1]
                    last = sc_.activation(dst.rearrange("p (n s) -> p n s", s=3)[:, :, s],
                                          U[:, 256 * s:256 * s + NP3], ACT.Identity, bias=bv,
                                          scale=D ** -0.5 if kind == "q" else 1.0)
                if kind == "v" and w >= 1:
                    last = diag_copy(w - 1)
                last.then_inc(s_ue, 1)

            def exps(u, i):
                n = 2 * NT * u + i
                b, j = divmod(u, NPAIR)
                act.wait_ge(s_max, n + 1)
                if i == 0 and j == 0 and b >= 2:
                    act.wait_ge(s_at, b - 1)
                sc_.activation(S[n % 3][:, 0:N], S[n % 3][:, 0:N], ACT.Exp, bias=nm[:, b % 2, j, i:i + 1],
                               accum_out=sm[:, b % 2, j, i:i + 1]).then_inc(s_exp, 1)

            def diag_exp(b):
                act.wait_ge(s_ex1, b + 1)
                sc_.activation(at[:, b % 2], at[:, b % 2], ACT.Exp).then_inc(s_ex2, 1)

            def extra(u, n):
                es = extras(u)
                if n >= len(es) or es[n] is None:
                    return
                kind, b, k = es[n]
                if kind == "t":
                    act.wait_ge(s_uf, unit_no[("t", b, 0)] + 1)
                    sc_.copy(xT2[:], U[0:D + 1, 0:NT * P]).then_inc(s_ue, 1)
                elif kind == "l":
                    act.wait_ge(s_uf, unit_no[("l", b, k)] + 1)
                    if b >= 1 and k == 0:
                        act.wait_ge(s_m7, b)
                    sc_.copy(L[:, 3 * k:3 * k + 3, :].rearrange("p t n -> p (t n)"),
                             U[:, 0:768]).then_inc(s_ue, 1)

            for w in range(AHEAD):
                for kind in "qkv":
                    qkv_out(kind, w)
            for u in range(NU + NPAIR):
                for i in range(2 * NT):
                    if u < NU:
                        exps(u, i)
                    if i in (1, 3, 5) and u + AHEAD < NU:
                        qkv_out("qkv"[i // 2], u + AHEAD)
                    if i == 5 and u + AHEAD == NU:
                        act.wait_ge(s_uf, unit_no[("d", NU - 1, 0)] + 1)
                        diag_copy(NU - 1).then_inc(s_ue, 1)
                    if i == 1 and u % NPAIR == 0 and u >= NPAIR:
                        diag_exp(u // NPAIR - 1)
                    if i in (7, 9, 11):
                        extra(u, (i - 7) // 2)
            act.wait_ge(s_abs, 1)
            sc_.activation(xrow[:, :, C_W:C_H], lg[:], ACT.Gelu).then_inc(s_gelu, 1)
            for k in range(F_TILES):
                act.wait_ge(s_zp, k + 1)
                if k >= 3:
                    act.wait_ge(s_y, k - 2)
                zp = S[0][:, 512 * (k % 2):512 * (k % 2) + 512]
                ep = S[1][0:32, 512 * (k % 2):512 * (k % 2) + P]
                sc_.copy(zT[:, k % 3, :], zp)
                sc_.copy(eT[:, k % 3, :], ep).then_inc(s_zc, 1)

        @block.vector
        def _(dve):
            v = nc.vector
            link = chain(dve, vs)

            def signs(b):
                dve.wait_ge(s_xin[b], 16)
                v.tensor_scalar(sgn[:, b * XB:(b + 1) * XB, :], xin[:, b * XB:(b + 1) * XB, :], 0.0, 0.5,
                                ALU.is_ge, ALU.subtract).then_inc(s_sgn, 1)

            signs(0)
            dve.wait_ge(s_par, 16 * 6)
            v.tensor_scalar(kq[:], kk[:], 0.0, 0.5, ALU.is_ge, ALU.subtract).then_inc(s_kq, 1)
            signs(1)
            for b in range(B):
                bt = slice(b * NT, (b + 1) * NT)
                if b + 2 < B:
                    signs(b + 2)
                if b == 0:
                    dve.wait_ge(s_bn, 1)
                dve.wait_ge(s_cv, b + 1)
                hv = xrow[:, bt, C_H:C_ID]
                cv = S[1][:, 512 * (b % 2):512 * (b % 2) + NT * D].rearrange("p (t d) -> p t d", t=NT)
                if b == 0:
                    dve.wait_ge(s_fill, 16)
                v.tensor_tensor(hv, cv, bnA[:].unsqueeze(1).to_broadcast([P, NT, D]), ALU.mult).then_inc(s_h, 1)
                dve.wait_ge(s_h, b + 1)
                link(v.tensor_tensor(hv, hv, bnC[:].unsqueeze(1).to_broadcast([P, NT, D]), ALU.add))
                link(v.tensor_reduce(ln1[:, 0, :], hv, X, ALU.add))
                link(v.tensor_scalar(ln1[:, 0, :], ln1[:, 0, :], -1.0 / D, None, ALU.mult))
                link(v.tensor_tensor(cent[:], hv, ln1[:, 0, :].unsqueeze(2).to_broadcast([P, NT, D]), ALU.add))
                if b >= 1:
                    dve.wait_ge(s_xhl, b)
                link(v.tensor_tensor(sq[:], cent[:], cent[:], ALU.mult))
                v.tensor_reduce(ln1[:, 1, :], sq[:], X, ALU.add).then_inc(s_sum, 1)
                dve.wait_ge(s_rs, b + 1)
                v.tensor_tensor(sq[:], cent[:], ln1[:, 3, :].unsqueeze(2).to_broadcast([P, NT, D]),
                                ALU.mult).then_inc(s_xn, 1)
                if b == 0:
                    dve.wait_ge(s_w, 32)
                    for g in range(3):
                        gs = slice(g * H * D, (g + 1) * H * D)
                        src = wst[:, gs].rearrange("p (d h) -> p h d", h=H)
                        hi = wq[:, 0, gs].rearrange("p (h d) -> p h d", h=H)
                        lo = wq[:, 1, gs].rearrange("p (h d) -> p h d", h=H)
                        link(v.tensor_copy(hi, src))
                        last = v.tensor_tensor(lo, src, hi, ALU.subtract)
                    last.then_inc(s_wq, 1)
                    dve.wait_ge(s_bq, 32)
                    for a in range(2):
                        hs = slice(a * D, (a + 1) * D)
                        ins = v.tensor_copy(bq[hs, :].rearrange("p (g j) -> p g j", g=3), bqn[hs, :, a::2])
                    link(ins)
                    v.tensor_scalar(bq8[:], bq[:], D ** -0.5, None, ALU.mult).then_inc(s_bn, 1)

            def hi_cast(kind, w):
                n = "qk".index(kind)
                dve.wait_ge(s_ue, unit_no[(kind, w, 0)] + 1)
                if w >= 2:
                    dve.wait_ge(s_st[(w - 2) % 3], 16 * 8 * ((w - 2) // 3 + 1))
                v.tensor_copy(hl[:, w % 2, n, 0, 0:QN], (q32, k32)[n][:, w % 2, 0:QN]).then_inc((s_qc, s_kc)[n], 1)

            def maxima(u, i):
                n = 2 * NT * u + i
                b, j = divmod(u, NPAIR)
                dve.wait_ge(s_score, n + 1)
                v.tensor_reduce(nm[:, b % 2, j, i:i + 1], S[n % 3][:, 0:N], X, ALU.max, negate=True).then_inc(s_max, 1)

            def diag_weights(b):
                dve.wait_ge(s_exp, 2 * NT * NPAIR * (b + 1))
                dve.wait_ge(s_ue, diag_unit(NPAIR * b + NPAIR - 1) + 1)
                v.reciprocal(sm[:, b % 2], sm[:, b % 2])
                v.tensor_tensor(at[:, b % 2], dg[:, b % 2], nm[:, b % 2], ALU.add).then_inc(s_ex1, 1)

            def diag_scale(b):
                dve.wait_ge(s_ex2, b + 1)
                link(v.tensor_tensor(at[:, b % 2], at[:, b % 2], sm[:, b % 2], ALU.mult))
                if b >= 1:
                    dve.wait_ge(s_axp, NPAIR * b)
                link(v.tensor_copy(ath[:, 0], at[:, b % 2]))
                v.tensor_tensor(ath[:, 1], at[:, b % 2], ath[:, 0], ALU.subtract).then_inc(s_at, 1)

            def extra(u, n):
                es = extras(u)
                if n >= len(es) or es[n] is None:
                    return
                kind, b, k = es[n]
                bt = slice(b * NT, (b + 1) * NT)
                if kind == "bc":
                    dve.wait_ge(s_uf, unit_no[("bc", b, k)] + 1)
                    if b >= 1 and k == 0:
                        dve.wait_ge(s_uf, unit_no[("o", b - 1, 0)] + 1)
                    c = START[-1]
                    e = (NT - 1) * P
                    vt = vT[:, (NPAIR * b + k) % 8, :]
                    v.tensor_tensor(avT[:, k, 0:e], vt[:, 0:e], U[:, 0:e], ALU.mult)
                    v.tensor_tensor(avT[:, k, e:], vt[:, c:N], U[:, e:NT * P], ALU.mult).then_inc(s_av, 1)
                    dve.wait_ge(s_av, NPAIR * b + k + 1)
                    dve.sem_inc(s_ue, 1)
                elif kind == "o":
                    dve.wait_ge(s_uf, unit_no[("o", b, 0)] + 1)
                    dve.wait_ge(s_hb, b + 1)
                    hv = xrow[:, bt, C_H:C_ID]
                    v.tensor_tensor(hv, U[:, 0:NT * D].rearrange("p (t d) -> p t d", t=NT), hv,
                                    ALU.add).then_inc(s_ue, 1)
                    dve.wait_ge(s_ue, unit_no[("o", b, 0)] + 1)
                    v.tensor_reduce(ln2[:, 0, :], hv, X, ALU.add).then_inc(s_h2, 1)
                elif kind == "r":
                    dve.wait_ge(s_uf, unit_no[("r", b, 0)] + 1)
                    rm = ML[:, :, 0:LEAVES]
                    v.tensor_tensor(rm, U[:, 0:NT * P].rearrange("p (t n) -> p t n", t=NT), m7[:, bt, :],
                                    ALU.mult).then_inc(s_ue, 1)
                    dve.wait_ge(s_ue, unit_no[("r", b, 0)] + 1)
                    v.tensor_reduce(rank[:, bt], rm, X, ALU.add).then_inc(s_rk, 1)

            def ln2_sumsq(b):
                dve.wait_ge(s_c2, b + 1)
                v.tensor_reduce(ln2[:, 1, :], sq[:], X, ALU.add).then_inc(s_ss2, 1)

            def path_logits(b):
                dve.wait_ge(s_ml, b + 1)
                for lv in range(DEPTH):
                    n = 2 ** lv
                    last = v.tensor_reduce(lg[:, b * NT:(b + 1) * NT, lv], ML[:, :, n - 1:2 * n - 1], X, ALU.add)
                last.then_inc(s_lg, 1)
                dve.wait_ge(s_lg, b + 1)

            for w in range(AHEAD):
                hi_cast("q", w)
                hi_cast("k", w)
            for u in range(NU + NPAIR):
                b, ph = u // NPAIR - 1, u % NPAIR
                for i in range(2 * NT):
                    if u < NU:
                        maxima(u, i)
                    if b >= 0 and ph == 0 and i == 0:
                        diag_weights(b)
                    if b >= 0 and ph == 0 and i == 2:
                        diag_scale(b)
                    if i in (2, 4) and u + AHEAD < NU:
                        hi_cast("qk"[i // 2 - 1], u + AHEAD)
                    if i in (7, 9, 11):
                        if b >= 0 and ph == 3 and i == 9:
                            path_logits(b)
                        extra(u, (i - 7) // 2)
                        if b >= 0 and ph == 1 and i == 11:
                            ln2_sumsq(b)

            lgb = sq[:].rearrange("p t d -> p (t d)")[:, 0:TT * (DEPTH - 1)].rearrange("p (t l) -> p t l", t=TT)
            dve.wait_ge(s_lg, B)
            dve.wait_ge(s_ss2, B)
            link(v.tensor_scalar(lgb, lg[:, :, 0:DEPTH - 1], 0.0, None, ALU.is_gt))
            link(v.tensor_tensor(lgb, lgb, pw2[:].unsqueeze(1).to_broadcast([P, TT, DEPTH - 1]), ALU.mult))
            link(v.tensor_reduce(leaf[:], lgb, X, ALU.add))
            v.scalar_tensor_tensor(lg[:], lg[:], -1.0, lg[:], ALU.mult, ALU.max).then_inc(s_abs, 1)
            dve.wait_ge(s_cnt, 1)
            link(v.tensor_scalar(ogi[:, 0:1], U[:, 0:1], -1.0, float(G - 1), ALU.add, ALU.max))
            link(v.tensor_scalar(ogi[:, 1:2], ogi[:, 0:1], 5, None, ALU.arith_shift_right))
            v.tensor_copy(og[:], ogi[:, 1:2]).then_inc(s_og, 1)
            dve.wait_ge(s_pre, 1)
            v.tensor_copy(ovb[:], U[:, 128:256])
            link(v.tensor_copy(endg[:], U[:, 256:257]))
            v.tensor_scalar(ind[:], giota[:], endg[:, 0:1], None, ALU.is_ge).then_inc(s_ind, 1)
            om = lm[:].rearrange("p a t n -> p (a t n)")[:, 0:TT * LEAVES].rearrange("p (t n) -> p t n", t=TT)
            link(v.tensor_tensor(om, m7[:], ovb[:].unsqueeze(1).to_broadcast([P, TT, LEAVES]), ALU.mult))
            link(v.tensor_reduce(sc[:, 0, :], om, X, ALU.add))
            link(v.tensor_scalar(sc[:, 0, :], sc[:, 0, :], float(G), float(STAT - G), ALU.mult, ALU.add))
            link(v.tensor_scalar(leaf[:], leaf[:], float(G), None, ALU.mult))
            link(v.tensor_tensor(sc[:, 0, :], sc[:, 0, :], leaf[:], ALU.subtract))
            link(v.tensor_scalar(sc[:, 1, :], rank[:], float(G), None, ALU.is_ge))
            link(v.tensor_tensor(sc[:, 0, :], sc[:, 0, :], sc[:, 1, :], ALU.mult))
            link(v.tensor_tensor(sc[:, 1, :], leaf[:], rank[:], ALU.add))
            link(v.tensor_tensor(sc[:, 2, :], sc[:, 0, :], sc[:, 1, :], ALU.add))
            link(v.tensor_scalar(sc[:, 3, 0:1], valid[:], -float(BIG), float(BIG), ALU.mult, ALU.add))
            dup = sc[:, 2, :].rearrange("p (b t) -> p b t", b=B)[:, :, NT - 1]
            link(v.tensor_scalar(dup, dup, sc[:, 3, 0:1], None, ALU.add))
            v.tensor_copy(slot[:], sc[:, 2, :]).then_inc(s_slot, 1)
            dve.wait_ge(s_lam, 1)
            link(v.tensor_scalar(lami[:, 0, :], U[0:1, 512:512 + OVG], float(LEAVES - 1), None, ALU.min))
            for i, sh in enumerate((0, 2, 4, 6)):
                link(v.tensor_scalar(lami[:, 1, :], lami[:, 0, :], sh, None, ALU.arith_shift_right))
                link(v.tensor_scalar(goff[:, :, i], lami[:, 1, :], float(D), float(PT[i] * D), ALU.mult, ALU.add))
            link(v.tensor_tensor(lami[:, 1, :], lami[:, 0, :], gpos[:], ALU.add))
            v.tensor_scalar(goff[:, :, 4], lami[:, 1, :], float(D), None, ALU.mult).then_inc(s_goff, 1)

            def make_z(k):
                if k % 4 == 0:
                    dve.wait_ge(s_xsr[k // 4 % NX], 16 * (k // 4 // NX + 1))
                if k >= 2:
                    dve.wait_ge(s_zp, k - 1)
                xk = xs[:, (k // 4) % NX, k % 4, :]
                wk = xk[:, C_W:C_H]
                v.tensor_tensor(z[:, k % 2, 0:DEPTH * D].rearrange("p (l d) -> p l d", l=DEPTH),
                                xk[:, 0:D].unsqueeze(1).to_broadcast([P, DEPTH, D]),
                                wk.unsqueeze(2).to_broadcast([P, DEPTH, D]), ALU.mult)
                v.tensor_tensor(z[:, k % 2, DEPTH * D:ZW].rearrange("p (g l) -> p g l", g=4),
                                wk.unsqueeze(1).to_broadcast([P, 4, DEPTH]),
                                gmask[:].unsqueeze(2).to_broadcast([P, 4, DEPTH]), ALU.mult).then_inc(s_z, 1)

            make_z(0)
            for k in range(F_TILES):
                if k + 1 < F_TILES:
                    make_z(k + 1)
                dve.wait_ge(s_y, k + 1)
                if k >= NO:
                    dve.wait_ge(s_outr[k % NO], 16 * (k // NO))
                xk = xs[:, (k // 4) % NX, k % 4, C_H:C_ID]
                if k < ST_TILES:
                    y = [S[2][:, 0:D], S[2][:, 512:512 + D]][k % 2]
                    v.tensor_tensor(yo[:, k % NO, :], y, xk, ALU.add).then_inc(s_yo, 1)
                else:
                    y = [S[2][:, 0:4 * D], S[2][:, 512:512 + 4 * D]][k % 2]
                    for g in range(4):
                        gs = slice(g * G, (g + 1) * G)
                        last = v.tensor_tensor(yo[gs, k % NO, :], y[gs, g * D:(g + 1) * D], xk[gs, :], ALU.add)
                    last.then_inc(s_yo, 1)


_INS = ["x", "L0_tok_kernel", "L0_tok_bias", "L0_tok_beta", "L0_tok_moving_mean", "L0_tok_moving_var",
        "L0_attn_Wqkv", "L0_attn_bqkv", "L0_attn_W0", "L0_attn_b0", "L0_ffn_w1s", "L0_ffn_b1s",
        "L0_ffn_w2s", "L0_ffn_b2s"]


def kernel(**inputs):
    import concourse.bacc as _bacc
    from concourse import mybir as _mybir
    from concourse.bass_utils import run_bass_kernel_spmd as _run

    nc = _bacc.Bacc("TRN2", target_bir_lowering=False, num_devices=1)
    arrays, args = {}, []
    for name in _INS:
        a = np.ascontiguousarray(inputs[name])
        arrays[f"in_{name}"] = a
        args.append(nc.dram_tensor(f"in_{name}", a.shape, _mybir.dt.from_np(a.dtype), kind="ExternalInput").ap())
    rows = nc.dram_tensor("sorted_rows", (SLOTS, RW), _mybir.dt.float32).ap()
    out = nc.dram_tensor("out_0", (B, N, D), _mybir.dt.float32, kind="ExternalOutput").ap()
    tower(nc, *args, rows, out, None)
    r = _run(nc, [arrays], core_ids=[0])
    return r.results[0]["out_0"]
```

```python
from contextlib import ExitStack

import numpy as np
import concourse.bass as bass
from concourse import mybir

B, NIN, CIN = 4, 750, 128
TAPS, D = 3, 64
N = NIN - TAPS + 1
H = 8
NPAIR = H // 2
DEPTH = 8
NODES = 2 ** DEPTH - 1
LEAVES = 2 ** (DEPTH - 1)
P = 128
NT = -(-N // P)
START = [min(t * P, N - P) for t in range(NT)]
DUP = NT * P - N
TT = B * NT
XP = 125
XB = NIN // XP
T = B * N
NP3 = 250
QN = 3 * NP3
PAD = QN + 2
XW = T + 2
G = 32
OVG = 96
STAT = LEAVES * G
SLOTS = STAT + OVG * G
ST_TILES, OV_TILES = STAT // P, OVG * G // P
F_TILES = ST_TILES + OV_TILES
C_ONE, C_W, C_H, C_ID = D, D + 1, D + 1 + DEPTH, 2 * D + 1 + DEPTH
RW = C_ID + 1
BIG = 1 << 20
LN_EPS, BN_EPS = 1e-5, 1e-3
PT = [42, 10, 2, 0]
PENT = 170


def tower(nc, x, k_tok, bias, beta, mean, var, Wqkv, bqkv, W0, b0, w1s, b1s, w2s, b2s, rows, out):
    f32, f16, bf16, i32, u32 = (mybir.dt.float32, mybir.dt.float16, mybir.dt.bfloat16,
                                mybir.dt.int32, mybir.dt.uint32)
    ALU = mybir.AluOpType
    ACT = mybir.ActivationFunctionType
    X = mybir.AxisListType.X
    ctx = ExitStack()
    with ctx:
        def sb(name, shape, dt=f32):
            return ctx.enter_context(nc.sbuf_tensor(name, shape, dt))

        def sem(name):
            return ctx.enter_context(nc.semaphore(name))

        wtab = sb("wtab", [P, PENT * D])
        pool_a = sb("pool_a", [P, 13 * PAD])
        st = pool_a[:, 0:6 * 3 * PAD // 2].bitcast(f16).rearrange("p (r a h n) -> p r a h n", r=3, a=3, h=2)
        qst, kst = st[:, :, 0], st[:, :, 1:3]
        hl0 = 6 * 3 * PAD // 2
        hl = pool_a[:, hl0:hl0 + 4 * PAD].bitcast(f16).rearrange("p (r k s n) -> p r k s n", r=2, k=2, s=2)
        btab = pool_a[0:32, 0:F_TILES * D].rearrange("p (k o) -> p k o", o=D)
        xhT = sb("xhT", [P, XW], f16)
        wq = sb("wq", [P, 2, 3 * H * D], f16)
        q32 = sb("q32", [P, 2, PAD])
        k32 = sb("k32", [P, 2, PAD])
        qk = sb("qk", [P, NT * P])
        vT = sb("vT", [P, 8, PAD])
        avT = sb("avT", [P, NPAIR, NT * P])
        xrow = sb("xrow", [P, TT, RW])
        xT2 = sb("xT2", [D + 1, NT * P])
        lm = sb("lm", [P, 2, NT, 256])
        L, M = lm[:, 0], lm[:, 1]
        ML = sb("ML", [P, NT, 256])
        gt = sb("gt", [P, NT, LEAVES])
        m7 = sb("m7", [P, TT, LEAVES], bf16)
        run = sb("run", [P, NT + 1, LEAVES], bf16)
        xin = lm[0:XP].rearrange("p a t n -> p (a t n)")[:, 0:B * XB * CIN].rearrange(
            "p (j c) -> p j c", c=CIN)
        sgn = avT[0:XP].rearrange("p j n -> p (j n)")[:, 0:B * XB * CIN // 2].bitcast(bf16).rearrange(
            "p (j c) -> p j c", c=CIN)
        wst = vT[:].rearrange("p j n -> p (j n)")[:, 0:3 * H * D]
        xT = ML[:].rearrange("p t n -> p (t n)")[:, 0:NIN].bitcast(bf16).rearrange("p (r n) -> p r n", r=2)
        cent = sb("cent", [P, NT, D])
        sq = sb("sq", [P, NT, D])
        xhl = sb("xhl", [P, NT, 2, D], f16)
        kk = sb("kk", [P, TAPS, D])
        kq = sb("kq", [P, TAPS, D], bf16)
        par = sb("par", [P, 5, D])
        bnA = sb("bnA", [P, D])
        bnC = sb("bnC", [P, D])
        half = sb("half", [P, D])
        bqn = sb("bqn", [P, 3, H])
        bq = sb("bq", [P, 12])
        bq8 = sb("bq8", [P, 12])
        w0p = sb("w0p", [P, NPAIR, D])
        w1n = sb("w1n", [P, 2, D])
        w1T = sb("w1T", [D + 1, 256])
        idf = sb("idf", [P, P])
        idb = sb("idb", [P, P], bf16)
        idh = sb("idh", [P, P], f16)
        tri = sb("tri", [P, P], bf16)
        tri_i = sb("tri_i", [P, P], bf16)
        ones = sb("ones", [P, P], bf16)
        sel = sb("sel", [P, 2])
        gmask = sb("gmask", [P, 4])
        valid = sb("valid", [P, NT])
        nm = sb("nm", [P, 2, NPAIR, 2 * NT])
        sm = sb("sm", [P, 2, NPAIR, 2 * NT])
        dg = sb("dg", [P, 2, NPAIR, 2 * NT])
        at = sb("at", [P, 2, NPAIR, 2 * NT])
        ath = sb("ath", [P, 2, NPAIR, 2 * NT], f16)
        ln1 = sb("ln1", [P, 4, NT])
        ln2 = sb("ln2", [P, 4, NT])
        lg = sb("lg", [P, TT, DEPTH])
        rank = sb("rank", [P, TT])
        leaf = sb("leaf", [P, TT])
        sc = sb("sc", [P, 4, TT])
        slot = sb("slot", [P, TT], i32)
        pw2 = sb("pw2", [P, DEPTH - 1])
        ogi = sb("ogi", [P, 2], i32)
        og = sb("og", [P, 1], bf16)
        endg = sb("endg", [P, OV_TILES])
        ovb = sb("ovb", [P, LEAVES], bf16)
        giota = sb("giota", [P, OVG])
        gmaskp = sb("gmaskp", [32, 4])
        shift = sb("shift", [32, OV_TILES], i32)
        lamp = sb("lamp", [32, OVG])
        oidx = sb("oidx", [32, 2, OV_TILES], i32)
        ind = sb("ind", [P, OVG], bf16)
        lami = sb("lami", [1, OVG], i32)
        act_f = sb("act_f", [1, OVG + 1])
        nact = sb("nact", [1, 1], i32)
        NX = 4
        xs = vT[:].rearrange("p j n -> p (j n)")[:, 0:NX * 4 * RW].rearrange("p (r t c) -> p r t c", r=NX, t=4)
        ZW = DEPTH * D + 32
        z0 = NX * 4 * RW
        z = vT[:].rearrange("p j n -> p (j n)")[:, z0:z0 + 3 * ZW].rearrange("p (r c) -> p r c", r=3)
        zT = avT[:].rearrange("p j n -> p (j n)")[:, 0:3 * 512].rearrange("p (r c) -> p r c", r=3)
        eT = avT[0:32].rearrange("p j n -> p (j n)")[:, 3 * 512:3 * 640].rearrange("p (r c) -> p r c", r=3)
        NO = 8
        yo = lm[:].rearrange("p a t n -> p (a t n)")[:, 0:NO * D].rearrange("p (r c) -> p r c", r=NO)

        S = [ctx.enter_context(nc.psum_tensor(f"S{i}", [P, 1024], f32)) for i in range(3)]
        U = ctx.enter_context(nc.psum_tensor("U", [P, 1024], f32))
        U_D = 1000

        def y_bank(k):
            return ([S[2], U][k // 2 % 2])[:, 512 * (k % 2):512 * (k % 2) + 512]

        (s_par, s_w, s_bq, s_w0, s_w1, s_b1, s_tab, s_btab, s_fill, s_id, s_seg) = [
            sem(n) for n in ("params_in", "wqkv_in", "bq_in", "w0_in", "w1_in",
                             "b1_in", "table_in", "btab_in", "rows_filled", "consts_ready", "scatter_done")]
        (s_sgn, s_xtp, s_xtc, s_cv, s_h, s_sum, s_rs, s_xn, s_hi, s_xhl, s_xhp, s_xhT, s_wq, s_bn, s_kq, s_w1p,
         s_w1c, s_hb) = [sem(n) for n in (
            "signs", "x_blocks_T", "x_blocks_copied", "conv_done", "h_ready", "ln_sums", "ln_rstd", "ln_x",
            "x_hi", "x_lo", "xhat_T", "xhat_copied", "wq_split", "bn_ready", "kq_ready", "w1_T", "w1_copied",
            "h_plus_b0")]
        (s_uf, s_ue, s_score, s_max, s_exp, s_qc, s_kc, s_lo, s_prod, s_av) = [sem(n) for n in (
            "unit_filled", "unit_emptied", "scores", "maxima", "exps", "qk_hi_q", "qk_hi_k", "qk_lo", "qk_prod",
            "av_ready")]
        s_xin = [sem(f"x_in{b}") for b in range(B)]
        s_xsr = [sem(f"rows_in{r}") for r in range(NX)]
        s_outr = [sem(f"out_written{r}") for r in range(NO)]
        s_st = [sem(f"stacks_in{r}") for r in range(3)]
        (s_ex1, s_ex2, s_at, s_h2, s_c2, s_ss2, s_xh2, s_ml, s_lg, s_m7, s_rk, s_gelu) = [sem(n) for n in (
            "diag_shifted", "diag_exp", "at_ready", "h2_ready", "ln2_squares", "ln2_sumsq", "xhat2_ready",
            "masked_logits", "path_logits", "leaf_masks", "ranks", "gelu_done")]
        (s_cnt, s_og, s_pre, s_ind, s_lam, s_goff, s_slot, s_abs, s_ovb) = [sem(n) for n in (
            "leaf_counts", "leaf_groups", "group_prefix", "group_index", "group_leaf", "group_offsets", "slots",
            "abs_logits", "ovb")]
        (s_z, s_zp, s_zc, s_y, s_yo) = [sem(n) for n in (
            "z_ready", "z_T", "zT_copied", "y_ready", "rows_out")]
        s_ob = [sem(f"overflow_bias_in{k}") for k in range(OV_TILES)]
        vs, ps_, as_ = sem("vector_step"), sem("pool_step"), sem("scalar_step")

        def chain(engine, s):
            n = [0]

            def link(ins):
                n[0] += 1
                ins.then_inc(s, 1)
                engine.wait_ge(s, n[0])
            return link

        def extras(u):
            b, ph = u // NPAIR - 1, u % NPAIR
            if b < 0:
                return []
            return [[("bc", b, 0), ("bc", b, 1), ("bc", b, 2)], [("bc", b, 3), ("o", b, 0)],
                    [("t", b, 0), ("l", b, 0), ("l", b, 1)], [None, None, ("r", b, 0)]][ph]

        NU = B * NPAIR
        AHEAD = 2
        units = [(k, w, 0) for w in range(AHEAD) for k in "qkv"]
        for u in range(NU + NPAIR):
            if u < NU and u + AHEAD < NU:
                units += [(k, u + AHEAD, 0) for k in "qkv"]
            if u + AHEAD == NU:
                units.append(("d", NU - 1, 0))
            units += [e for e in extras(u) if e]
        unit_no = {k: n for n, k in enumerate(units)}

        def diag_unit(w):
            return unit_no[("v", w + 1, 0) if w + 1 < NU else ("d", w, 0)]

        def routing(b, eng, ops, link):
            eng.wait_ge(s_ue, unit_no[("l", b, 1)] + 1)
            if b >= 1:
                eng.wait_ge(s_lg, b)
            link(ops.memset(M[:, :, 0:1], 1.0))
            link(ops.tensor_scalar(gt[:, :, 0:LEAVES - 1], L[:, :, 0:LEAVES - 1], 0.0, None, ALU.is_gt))
            for lv in range(DEPTH - 1):
                n = 2 ** lv
                par_ = M[:, :, n - 1:2 * n - 1]
                kid = M[:, :, 2 * n - 1:4 * n - 1].rearrange("p t (n c) -> p t n c", c=2)
                link(ops.tensor_tensor(kid[:, :, :, 1], par_, gt[:, :, n - 1:2 * n - 1], ALU.mult))
                link(ops.tensor_tensor(kid[:, :, :, 0], par_, kid[:, :, :, 1], ALU.subtract))
            if b >= 1:
                eng.wait_ge(s_rk, b)
            ops.tensor_tensor(ML[:, :, 0:NODES], M[:, :, 0:NODES], L[:, :, 0:NODES], ALU.mult).then_inc(s_ml, 1)
            t0 = b * NT
            link(ops.tensor_tensor(m7[:, t0:t0 + NT, :], M[:, :, LEAVES - 1:NODES],
                                   valid[:].unsqueeze(2).to_broadcast([P, NT, LEAVES]), ALU.mult))
            if b >= 1:
                link(ops.tensor_tensor(run[:, 0, :], run[:, NT, :], ones[:], ALU.mult))
            for j in range(NT):
                link(ops.tensor_tensor(run[:, j + 1, :], run[:, j, :], m7[:, t0 + j, :], ALU.add))
            eng.sem_inc(s_m7, 1)

        block = ctx.enter_context(nc.Block())

        @block.sync
        def _(sp):
            xv = x.rearrange("b (j p) c -> p (b j) c", p=XP)
            for b in range(B):
                sp.dma_start(xin[:, b * XB:(b + 1) * XB, :], xv[:, b * XB:(b + 1) * XB, :]).then_inc(s_xin[b], 16)
                if b == 0:
                    sp.dma_start(kk[:], k_tok.rearrange("t c o -> c t o")).then_inc(s_par, 16)
                    for n, v in enumerate((bias, beta, mean, var, b0)):
                        sp.dma_start(par[:, n, :], v.partition_broadcast(P)).then_inc(s_par, 16)
            sp.dma_start(wst[0:D, :], Wqkv).then_inc(s_w, 16)
            sp.dma_start(wst[D:P, :], Wqkv).then_inc(s_w, 16)
            for a in range(2):
                sp.dma_start(bqn[a * D:(a + 1) * D], bqkv.rearrange("(g d h) -> d g h", g=3, d=D)).then_inc(s_bq, 16)
            w0v = W0.rearrange("(d j a) o -> a d j o", j=NPAIR, a=2)
            for a in range(2):
                sp.dma_start(w0p[a * D:(a + 1) * D, :, :], w0v[a]).then_inc(s_w0, 16)
            sp.dma_start(w1n[:, 0, :], w1s[0:P, :]).then_inc(s_w1, 16)
            sp.dma_start(w1n[0:NODES - P, 1, :], w1s[P:NODES, :]).then_inc(s_w1, 16)
            sp.dma_start(w1T[D:D + 1, 0:NODES], b1s.unsqueeze(0)).then_inc(s_b1, 16)
            sp.wait_ge(s_id, 1)
            sp.dma_start(rows.rearrange("(t p) c -> p t c", p=P),
                         xrow[:, 0:1, :].to_broadcast([P, F_TILES, RW])).then_inc(s_fill, 16)
            tv = wtab[:].rearrange("p (e o) -> p e o", o=D)
            wv = w2s.rearrange("n d o -> d n o")
            for i, lv in enumerate((6, 4, 2, 0)):
                n = 2 ** lv
                dst = tv[0:D, PT[i]:PT[i] + 2 * n, :].rearrange("p (e r) o -> p e r o", r=2)
                for r in range(2):
                    sp.dma_start(dst[:, :, r, :], wv[:, n - 1:2 * n - 1, :]).then_inc(s_tab, 16)
                sp.dma_start(tv[D:P, PT[i]:PT[i] + 2 * n, :], wv[:, 2 * n - 1:4 * n - 1, :]).then_inc(s_tab, 16)
            for w in range(NU):
                r, c = w % 3, w % 2
                sp.wait_ge(s_lo, 2 * w + 2)
                if w >= 3:
                    sp.wait_ge(s_score, 2 * NT * (w - 2))
                for a in range(2):
                    src = slice(a * D, (a + 1) * D)
                    for half_ in range(2):
                        dst = slice(half_ * D, (half_ + 1) * D)
                        sp.dma_start(qst[dst, r, a, 0:QN], hl[src, c, 0, half_, 0:QN]).then_inc(s_st[r], 16)
                        sp.dma_start(kst[dst, r, :, a, 0:QN], hl[src, c, 1, :, 0:QN]).then_inc(s_st[r], 16)
            sp.wait_ge(s_score, 2 * NT * NU)
            for g in range(4):
                for lv in range(DEPTH):
                    row = btab[g * 8 + lv:g * 8 + lv + 1, 0:ST_TILES, :]
                    first = 2 ** lv - 1
                    if lv <= 5:
                        n, rep = 2 ** lv, ST_TILES // 2 ** lv
                        src = b2s[first:first + n, :].unsqueeze(0).unsqueeze(2).to_broadcast([1, n, rep, D])
                        row = row.rearrange("p (n r) o -> p n r o", r=rep)
                    else:
                        m = 2 ** (lv - 5)
                        src = b2s[first:first + m * ST_TILES, :].rearrange("(a k m) o -> m a k o", a=1, m=m)[g * m // 4]
                    sp.dma_start(row, src).then_inc(s_btab, 16)
            rv = rows.rearrange("(t p) c -> p t c", p=P)
            sp.wait_ge(s_seg, 16 * TT)
            def load_rows(k):
                if k >= NX:
                    for t in range(4 * (k - NX), 4 * (k - NX) + 4):
                        sp.wait_ge(s_outr[t % NO], 16 * (t // NO + 1))
                sp.dma_start(xs[:, k % NX], rv[:, 4 * k:4 * k + 4, :]).then_inc(s_xsr[k % NX], 16)

            for k in range(ST_TILES // 4):
                load_rows(k)
            sp.wait_ge(s_goff, 1)
            groups = sp.value_load(nact[0:1, 0:1], min_val=0, max_val=OVG)
            for k in range(ST_TILES // 4, F_TILES // 4):
                with sp.If(groups > 4 * (4 * k - ST_TILES)):
                    load_rows(k)
            for k in range(ST_TILES - NO, ST_TILES):
                sp.wait_ge(s_outr[k % NO], 16 * (k // NO + 1))
            for k in range(ST_TILES, F_TILES):
                with sp.If(groups > 4 * (k - ST_TILES)):
                    sp.wait_ge(s_outr[k % NO], 16 * (k // NO + 1))

        @block.gpsimd
        def _(pool):
            gp = nc.gpsimd
            link = chain(pool, ps_)
            gp.memset(half[:], -0.5)
            gp.memset(ones[:], 1.0)
            gp.memset(xrow[:], 0.0)
            gp.memset(xhT[:, T:XW], 0.0)
            gp.memset(run[:, 0, :], 0.0)
            gp.memset(sel[:], 0.0)
            gp.memset(gmask[:], 1.0)
            gp.memset(valid[:], 1.0)
            gp.memset(idf[:], 0.0)
            link(gp.memset(tri[:], 1.0))
            link(gp.affine_select(out=idf[:], in_=idf[:], compare_op=ALU.not_equal, fill=1.0, base=0,
                                  pattern=[[-1, P]], channel_multiplier=1))
            link(gp.memset(sel[0:D, 0:1], 1.0))
            link(gp.memset(sel[D:P, 1:2], 1.0))
            gp.affine_select(out=valid[:, NT - 1:NT], in_=valid[:, NT - 1:NT], compare_op=ALU.is_ge, fill=0.0,
                             base=-DUP, pattern=[[0, 1]], channel_multiplier=1)
            link(gp.affine_select(out=gmask[:], in_=gmask[:], compare_op=ALU.is_ge, fill=0.0, base=0,
                                  pattern=[[-G, 4]], channel_multiplier=1))
            link(gp.affine_select(out=gmask[:], in_=gmask[:], compare_op=ALU.is_ge, fill=0.0, base=G - 1,
                                  pattern=[[G, 4]], channel_multiplier=-1))
            link(gp.memset(gmaskp[:], 1.0))
            link(gp.affine_select(out=gmaskp[:], in_=gmaskp[:], compare_op=ALU.is_ge, fill=0.0, base=0,
                                  pattern=[[-8, 4]], channel_multiplier=1))
            link(gp.affine_select(out=gmaskp[:], in_=gmaskp[:], compare_op=ALU.is_ge, fill=0.0, base=7,
                                  pattern=[[8, 4]], channel_multiplier=-1))
            link(gp.iota(shift[:], pattern=[[0, OV_TILES]], base=0, channel_multiplier=1))
            gp.tensor_copy(idb[:], idf[:])
            gp.tensor_copy(idh[:], idf[:])
            gp.affine_select(out=tri_i[:], in_=tri[:], compare_op=ALU.is_ge, fill=0.0, base=0,
                             pattern=[[1, P]], channel_multiplier=-1)
            link(gp.affine_select(out=tri[:], in_=tri[:], compare_op=ALU.is_gt, fill=0.0, base=0,
                                  pattern=[[1, P]], channel_multiplier=-1))
            gp.iota(giota[:], pattern=[[1, OVG]], base=0, channel_multiplier=0, allow_small_or_imprecise_dtypes=True)
            for lv in range(DEPTH - 1):
                gp.memset(pw2[:, lv:lv + 1], float(2 ** (DEPTH - 2 - lv)))
            link(gp.memset(xrow[:, 0, C_ID:C_ID + 1].bitcast(i32), BIG))
            link(gp.memset(w1T[D:D + 1, NODES:256], 0.0))
            pool.sem_inc(s_id, 1)
            pool.wait_ge(s_par, 16 * 6)
            link(gp.tensor_scalar(bnA[:], par[:, 3, :], BN_EPS, 1.0, ALU.add, ALU.mult))
            link(gp.tensor_tensor(bnA[:], bnA[:], half[:], ALU.pow))
            link(gp.tensor_tensor(bnC[:], par[:, 0, :], par[:, 2, :], ALU.subtract))
            link(gp.tensor_tensor(bnC[:], bnC[:], bnA[:], ALU.mult))
            link(gp.tensor_tensor(bnC[:], bnC[:], par[:, 1, :], ALU.add))
            gp.tensor_scalar(bnA[:], bnA[:], 4.0, 0.0, ALU.mult, ALU.add).then_inc(s_bn, 1)
            pool.wait_ge(s_fill, 16)
            for t in range(TT):
                b, j = divmod(t, NT)
                gp.iota(xrow[:, t, C_ID:C_ID + 1].bitcast(i32), pattern=[[0, 1]], base=b * N + START[j],
                        channel_multiplier=1)
            link(gp.memset(xrow[:, :, C_ONE:C_ONE + 1], 1.0))

            for b in range(B):
                bt = slice(b * NT, (b + 1) * NT)
                pool.wait_ge(s_sum, b + 1)
                link(gp.tensor_scalar(ln1[:, 2, :], ln1[:, 1, :], 1.0 / D, LN_EPS, ALU.mult, ALU.add))
                gp.tensor_tensor(ln1[:, 3, :], ln1[:, 2, :], half[:, 0:NT], ALU.pow).then_inc(s_rs, 1)
                pool.wait_ge(s_hi, b + 1)
                gp.tensor_tensor(xhl[:, :, 1, :], sq[:], xhl[:, :, 0, :], ALU.subtract).then_inc(s_xhl, 1)
                gp.tensor_tensor(xrow[:, bt, C_H:C_ID], xrow[:, bt, C_H:C_ID],
                                 par[:, 4:5, :].to_broadcast([P, NT, D]), ALU.add).then_inc(s_hb, 1)

            def qk_lo(w):
                c = w % 2
                for n, (src, s_c) in enumerate(((q32, s_qc), (k32, s_kc))):
                    pool.wait_ge(s_c, w + 1)
                    gp.tensor_tensor(hl[:, c, n, 1, 0:QN], src[:, c, 0:QN], hl[:, c, n, 0, 0:QN],
                                     ALU.subtract).then_inc(s_lo, 1)
                if w >= 1:
                    pool.wait_ge(s_uf, diag_unit(w - 1) + 1)
                gp.tensor_tensor(qk[:, 0:N], q32[:, c, 0:N], k32[:, c, 0:N], ALU.mult).then_inc(s_prod, 1)

            def ln2_squares(b):
                pool.wait_ge(s_h2, b + 1)
                bt = slice(b * NT, (b + 1) * NT)
                link(gp.tensor_scalar(ln2[:, 2, :], ln2[:, 0, :], -1.0 / D, 0.0, ALU.mult, ALU.add))
                link(gp.tensor_tensor(cent[:], xrow[:, bt, C_H:C_ID],
                                      ln2[:, 2, :].unsqueeze(2).to_broadcast([P, NT, D]), ALU.add))
                gp.tensor_tensor(sq[:], cent[:], cent[:], ALU.mult).then_inc(s_c2, 1)

            def ln2_x(b):
                pool.wait_ge(s_ss2, b + 1)
                bt = slice(b * NT, (b + 1) * NT)
                link(gp.tensor_scalar(ln2[:, 2, :], ln2[:, 1, :], 1.0 / D, LN_EPS, ALU.mult, ALU.add))
                link(gp.tensor_tensor(ln2[:, 3, :], ln2[:, 2, :], half[:, 0:NT], ALU.pow))
                gp.tensor_tensor(xrow[:, bt, 0:D], cent[:],
                                 ln2[:, 3, :].unsqueeze(2).to_broadcast([P, NT, D]), ALU.mult).then_inc(s_xh2, 1)

            for w in range(AHEAD):
                qk_lo(w)
            for u in range(NU + NPAIR):
                b, ph = u // NPAIR - 1, u % NPAIR
                if 0 <= b < B - 1 and ph == 3:
                    routing(b, pool, gp, link)
                if u + AHEAD < NU:
                    qk_lo(u + AHEAD)
                if b >= 0 and ph == 1:
                    ln2_squares(b)
                    ln2_x(b)
            pool.wait_ge(s_slot, 1)
            pool.wait_ge(s_gelu, 1)
            for t in range(TT):
                gp.indirect_dma_start(rows, bass.IndirectOffsetOnAxis(slot[:, t:t + 1].bitcast(u32), 0),
                                      xrow[:, t, :], None, bounds_check=SLOTS - 1,
                                      oob_is_err=False).then_inc(s_seg, 16)
            outf = out.rearrange("b n o -> (b n) o")
            pool.wait_ge(s_goff, 1)
            groups = pool.value_load(nact[0:1, 0:1], min_val=0, max_val=OVG)

            def overflow_bias(kk):
                gp.indirect_dma_start(btab[:, ST_TILES + kk, :], None, b2s,
                                      bass.IndirectOffsetOnAxis(oidx[:, 0, kk:kk + 1].bitcast(u32), 0),
                                      bounds_check=NODES - 1, oob_is_err=False).then_inc(s_ob[kk], 16)

            def rows_out(k):
                pool.wait_ge(s_yo, k + 1)
                ids = xs[:, (k // 4) % NX, k % 4, C_ID:C_ID + 1]
                gp.indirect_dma_start(outf, bass.IndirectOffsetOnAxis(ids.bitcast(u32), 0), yo[:, k % NO, :], None,
                                      bounds_check=T - 1, oob_is_err=False).then_inc(s_outr[k % NO], 16)

            for k in range(ST_TILES):
                rows_out(k)
                if k < OV_TILES:
                    with pool.If(groups > 4 * k):
                        overflow_bias(k)
            for k in range(ST_TILES, F_TILES):
                with pool.If(groups > 4 * (k - ST_TILES)):
                    rows_out(k)

        @block.tensor
        def _(pe):
            mm = nc.tensor.matmul
            pe.wait_ge(s_id, 1)
            pe.wait_ge(s_w1, 32)
            nc.tensor.transpose(U[0:D, 0:P], w1n[:, 0, :], idf[:])
            nc.tensor.transpose(U[0:D, P:NODES], w1n[0:NODES - P, 1, :],
                                idf[0:NODES - P, 0:NODES - P]).then_inc(s_w1p, 1)

            def x_blocks(b):
                pe.wait_ge(s_sgn, b + 1)
                if b >= 2:
                    pe.wait_ge(s_xtc, b - 1)
                xp = S[0][:, 512 * (b % 2):512 * (b % 2) + 384].bitcast(bf16).rearrange("p (j n) -> p j n", j=XB)
                for j in range(XB):
                    last = nc.tensor.transpose(xp[:, j, 0:XP], sgn[:, b * XB + j, :], idb[0:XP, 0:XP])
                last.then_inc(s_xtp, 1)

            def conv(b):
                pe.wait_ge(s_xtc, b + 1)
                pe.wait_ge(s_kq, 1)
                if b >= 2:
                    pe.wait_ge(s_h, b - 1)
                for j in range(NT):
                    o = 512 * (b % 2) + j * D
                    for k in range(TAPS):
                        last = mm(S[1][:, o:o + D], xT[:, b % 2, START[j] + k:START[j] + k + P], kq[:, k, :],
                                  start=(k == 0), stop=(k == TAPS - 1))
                last.then_inc(s_cv, 1)

            def xhat_T(b):
                pe.wait_ge(s_xhl, b + 1)
                if b >= 2:
                    pe.wait_ge(s_xhT, b - 1)
                xp = S[2][:, 512 * (b % 2):512 * (b % 2) + 384].bitcast(f16)
                for j in range(NT):
                    last = nc.tensor.transpose(xp[:, j * P:(j + 1) * P], xhl[:, j].rearrange("p a d -> p (a d)"),
                                               idh[:])
                last.then_inc(s_xhp, 1)

            x_blocks(0)
            x_blocks(1)
            for b in range(B):
                conv(b)
                if b + 2 < B:
                    x_blocks(b + 2)
                xhat_T(b)

            def fill(unit):
                if unit_no[unit]:
                    pe.wait_ge(s_ue, unit_no[unit])

            def project(kind, w):
                b, j = divmod(w, NPAIR)
                fill((kind, w, 0))
                base = "qkv".index(kind) * T + b * N
                for s in range(3):
                    r0, g = divmod(base + s, 3)
                    for a in range(2):
                        last = mm(U[:, 256 * s:256 * s + NP3], wq[:, a, g * H * D + j * P:g * H * D + (j + 1) * P],
                                  xhT[:, r0:r0 + NP3], start=(a == 0), stop=(a == 1))
                if kind == "v" and w >= 1:
                    last = diagonal(w - 1)
                last.then_inc(s_uf, 1)

            def diagonal(w):
                pe.wait_ge(s_prod, w + 1)
                for t in range(NT):
                    last = mm(U[:, U_D + t:U_D + t + NT + 1:NT], qk[:, START[t]:START[t] + P], sel[:],
                              start=True, stop=True)
                return last

            def broadcast(b, j):
                if j == 0:
                    pe.wait_ge(s_at, b + 1)
                fill(("bc", b, j))
                for t in range(NT):
                    for a in range(2):
                        for hd in range(2):
                            i = hd * NT + t
                            last = mm(U[hd * D:(hd + 1) * D, t * P:(t + 1) * P],
                                      ath[:, a, j, i:i + 1].to_broadcast([P, D]), idh[:],
                                      start=(a == 0), stop=(a == 1))
                last.then_inc(s_uf, 1)

            def out_proj(b):
                if b == 0:
                    pe.wait_ge(s_w0, 32)
                pe.wait_ge(s_av, NPAIR * (b + 1))
                fill(("o", b, 0))
                for t in range(NT):
                    for j in range(NPAIR):
                        last = mm(U[:, t * D:(t + 1) * D], avT[:, j, t * P:(t + 1) * P], w0p[:, j, :],
                                  start=(j == 0), stop=(j == NPAIR - 1))
                last.then_inc(s_uf, 1)

            def x2_T(b):
                pe.wait_ge(s_xh2, b + 1)
                fill(("t", b, 0))
                for t in range(NT):
                    last = nc.tensor.transpose(U[0:D + 1, t * P:(t + 1) * P], xrow[:, b * NT + t, 0:D + 1], idf[:])
                last.then_inc(s_uf, 1)

            def logits(b, n):
                fill(("l", b, n))
                if n == 0:
                    pe.wait_ge(s_w1c, 1)
                    pe.wait_ge(s_b1, 16)
                for t in range(3):
                    last = mm(U[:, t * 256:(t + 1) * 256], xT2[:, (3 * n + t) * P:(3 * n + t + 1) * P], w1T[:],
                              start=True, stop=True)
                last.then_inc(s_uf, 1)

            def ranks(b):
                pe.wait_ge(s_m7, b + 1)
                fill(("r", b, 0))
                for t in range(NT):
                    mm(U[:, t * P:(t + 1) * P], tri[:], m7[:, b * NT + t, :], start=True, stop=False)
                    last = mm(U[:, t * P:(t + 1) * P], ones[:], run[:, t, :], start=False, stop=True)
                last.then_inc(s_uf, 1)

            def extra(u, n):
                es = extras(u)
                if n >= len(es) or es[n] is None:
                    return
                kind, b, k = es[n]
                if kind == "bc":
                    broadcast(b, k)
                elif kind == "o":
                    out_proj(b)
                elif kind == "t":
                    x2_T(b)
                elif kind == "l":
                    logits(b, k)
                else:
                    ranks(b)

            def scores(u, i):
                hd, t = divmod(i, NT)
                n = 2 * NT * u + i
                if i == 0:
                    pe.wait_ge(s_st[u % 3], 16 * 8 * (u // 3 + 1))
                if n >= 3:
                    pe.wait_ge(s_exp, n - 2)
                for a in range(2):
                    for c0, c1 in ((0, 512), (512, N)):
                        last = mm(S[n % 3][:, c0:c1], kst[:, u % 3, a, hd, START[t]:START[t] + P],
                                  qst[:, u % 3, hd, c0:c1], start=(a == 0), stop=(a == 1))
                last.then_inc(s_score, 1)

            pe.wait_ge(s_xhT, B)
            pe.wait_ge(s_wq, 1)
            pe.wait_ge(s_w1c, 1)
            for w in range(AHEAD):
                for kind in "qkv":
                    project(kind, w)
            for u in range(NU + NPAIR):
                for i in range(2 * NT):
                    if u < NU:
                        scores(u, i)
                    if i in (1, 3, 5) and u + AHEAD < NU:
                        project("qkv"[i // 2], u + AHEAD)
                    if i == 5 and u + AHEAD == NU:
                        fill(("d", NU - 1, 0))
                        diagonal(NU - 1).then_inc(s_uf, 1)
                    if i in (7, 9, 11):
                        extra(u, (i - 7) // 2)
            pe.wait_ge(s_m7, B)
            pe.wait_ge(s_ue, len(units))
            mm(U[:, 0:1], run[:, NT, :], ones[:, 0:1], start=True, stop=True).then_inc(s_cnt, 1)
            pe.wait_ge(s_og, 1)
            mm(U[:, 128:256], og[:].to_broadcast([P, P]), tri[:], start=True, stop=True)
            mm(U[:, 256:257], tri_i[:], og[:], start=True, stop=True).then_inc(s_pre, 1)
            pe.wait_ge(s_ind, 1)
            mm(U[0:32, 512:512 + OVG], ones[:, 0:32], ind[:], start=True, stop=True).then_inc(s_lam, 1)

            tv = wtab[:].rearrange("p (e o) -> p e o", o=D)
            pe.wait_ge(s_tab, 16 * 12)
            pe.wait_ge(s_btab, 16 * 32)

            def z_T(k):
                pe.wait_ge(s_z, k + 1)
                if k >= 2:
                    pe.wait_ge(s_zc, k - 1)
                zp = S[0][:, 512 * (k % 2):512 * (k % 2) + 512]
                ep = S[1][0:32, 512 * (k % 2):512 * (k % 2) + P]
                for i in range(4):
                    nc.tensor.transpose(zp[:, i * P:(i + 1) * P], z[:, k % 3, i * P:(i + 1) * P], idf[:])
                nc.tensor.transpose(ep, z[:, k % 3, 512:ZW], idf[:]).then_inc(s_zp, 1)

            def tile_products(k):
                pe.wait_ge(s_zc, k + 1)
                if k >= 4:
                    pe.wait_ge(s_yo, k - 3)
                y = y_bank(k)[:, 0:D]
                for i, e in enumerate((PT[3] + k // 16, PT[2] + k // 4, PT[1] + k)):
                    mm(y, zT[:, k % 3, i * P:(i + 1) * P], tv[:, e, :], start=(i == 0), stop=False)
                mm(y, eT[:, k % 3, :], btab[:, k, :], start=False, stop=False)
                for g in range(4):
                    last = mm(y[g * G:(g + 1) * G, :], zT[:, k % 3, 3 * P + g * G:3 * P + (g + 1) * G],
                              tv[:, PT[0] + 4 * k + g, :], start=False, stop=True)
                last.then_inc(s_y, 1)

            def overflow_products(k):
                kk = k - ST_TILES
                leaves = [nc.tensor.value_load(lami[0:1, 4 * kk + g:4 * kk + g + 1], min_val=0,
                                               max_val=LEAVES - 1) for g in range(4)]
                pe.wait_ge(s_zc, k + 1)
                pe.wait_ge(s_yo, k - 3)
                pe.wait_ge(s_ob[kk], 16)
                y = y_bank(k)
                mm(y[:, 4 * D:5 * D], eT[:, k % 3, :], btab[:, k, :], start=True, stop=True)
                for g in range(4):
                    for i in range(4):
                        e = (leaves[g] >> (6 - 2 * i)) * D + PT[3 - i] * D
                        last = mm(y[0:G, g * D:(g + 1) * D], zT[:, k % 3, i * P + g * G:i * P + (g + 1) * G],
                                  wtab[:, bass.ds(e, D)], start=(i == 0), stop=(i == 3))
                last.then_inc(s_y, 1)

            z_T(0)
            for k in range(ST_TILES - 1):
                z_T(k + 1)
                tile_products(k)
            pe.wait_ge(s_goff, 1)
            groups = pe.value_load(nact[0:1, 0:1], min_val=0, max_val=OVG)
            for k in range(ST_TILES - 1, F_TILES):
                if k + 1 < F_TILES:
                    with pe.If(groups > 4 * (k + 1 - ST_TILES)):
                        z_T(k + 1)
                if k < ST_TILES:
                    tile_products(k)
                else:
                    with pe.If(groups > 4 * (k - ST_TILES)):
                        overflow_products(k)

        @block.scalar
        def _(act):
            sc_ = nc.scalar
            act.wait_ge(s_w1p, 1)
            sc_.copy(w1T[0:D, 0:NODES], U[0:D, 0:NODES])
            act.wait_ge(s_id, 1)
            sc_.mul(w1T[0:D, NODES:256], idf[0:D, 0:1], 0.0).then_inc(s_w1c, 1)

            def x_copy(b):
                act.wait_ge(s_xtp, b + 1)
                if b >= 2:
                    act.wait_ge(s_cv, b - 1)
                xp = S[0][:, 512 * (b % 2):512 * (b % 2) + 384].bitcast(bf16).rearrange("p (j n) -> p j n", j=XB)
                sc_.copy(xT[:, b % 2, :].rearrange("p (j n) -> p j n", j=XB), xp[:, :, 0:XP]).then_inc(s_xtc, 1)

            x_copy(0)
            x_copy(1)
            for b in range(B):
                act.wait_ge(s_xn, b + 1)
                if b >= 1:
                    act.wait_ge(s_xhp, b)
                sc_.copy(xhl[:, :, 0, :], sq[:]).then_inc(s_hi, 1)
                if b + 2 < B:
                    x_copy(b + 2)
                act.wait_ge(s_xhp, b + 1)
                xp = S[2][:, 512 * (b % 2):512 * (b % 2) + 384].bitcast(f16)
                sc_.copy(xhT[:, b * N:b * N + START[-1]], xp[:, 0:START[-1]])
                sc_.copy(xhT[:, b * N + START[-1]:(b + 1) * N], xp[:, (NT - 1) * P:]).then_inc(s_xhT, 1)

            def diag_copy(w):
                b, j = divmod(w, NPAIR)
                if b >= 2 and j == 0:
                    act.wait_ge(s_ex1, b - 1)
                return sc_.copy(dg[:, b % 2, j, :], U[:, U_D:U_D + 2 * NT])

            def qkv_out(kind, w):
                b, j = divmod(w, NPAIR)
                if w == 0:
                    act.wait_ge(s_bn, 2)
                act.wait_ge(s_uf, unit_no[(kind, w, 0)] + 1)
                if kind != "v" and w >= 2:
                    act.wait_ge(s_prod, w - 1)
                if kind == "v" and w >= 8:
                    act.wait_ge(s_av, w - 7)
                dst = {"q": q32[:, w % 2, 0:QN], "k": k32[:, w % 2, 0:QN], "v": vT[:, w % 8, 0:QN]}[kind]
                base = "qkv".index(kind) * T + b * N
                for s in range(3):
                    g = (base + s) % 3
                    bv = (bq8 if kind == "q" else bq)[:, g * NPAIR + j:g * NPAIR + j + 1]
                    last = sc_.activation(dst.rearrange("p (n s) -> p n s", s=3)[:, :, s],
                                          U[:, 256 * s:256 * s + NP3], ACT.Identity, bias=bv,
                                          scale=D ** -0.5 if kind == "q" else 1.0)
                if kind == "v" and w >= 1:
                    last = diag_copy(w - 1)
                last.then_inc(s_ue, 1)

            def exps(u, i):
                n = 2 * NT * u + i
                b, j = divmod(u, NPAIR)
                act.wait_ge(s_max, n + 1)
                if i == 0 and j == 0 and b >= 2:
                    act.wait_ge(s_at, b - 1)
                sc_.activation(S[n % 3][:, 0:N], S[n % 3][:, 0:N], ACT.Exp, bias=nm[:, b % 2, j, i:i + 1],
                               accum_out=sm[:, b % 2, j, i:i + 1]).then_inc(s_exp, 1)

            def diag_exp(b):
                act.wait_ge(s_ex1, b + 1)
                sc_.activation(at[:, b % 2], at[:, b % 2], ACT.Exp).then_inc(s_ex2, 1)

            def extra(u, n):
                es = extras(u)
                if n >= len(es) or es[n] is None:
                    return
                kind, b, k = es[n]
                if kind == "t":
                    act.wait_ge(s_uf, unit_no[("t", b, 0)] + 1)
                    sc_.copy(xT2[:], U[0:D + 1, 0:NT * P]).then_inc(s_ue, 1)
                elif kind == "l":
                    act.wait_ge(s_uf, unit_no[("l", b, k)] + 1)
                    if b >= 1 and k == 0:
                        act.wait_ge(s_m7, b)
                    sc_.copy(L[:, 3 * k:3 * k + 3, :].rearrange("p t n -> p (t n)"),
                             U[:, 0:768]).then_inc(s_ue, 1)

            for w in range(AHEAD):
                for kind in "qkv":
                    qkv_out(kind, w)
            for u in range(NU + NPAIR):
                for i in range(2 * NT):
                    if u < NU:
                        exps(u, i)
                    if i in (0, 2, 4) and u + AHEAD < NU:
                        qkv_out("qkv"[i // 2], u + AHEAD)
                    if i == 4 and u + AHEAD == NU:
                        act.wait_ge(s_uf, unit_no[("d", NU - 1, 0)] + 1)
                        diag_copy(NU - 1).then_inc(s_ue, 1)
                    if i == 2 and u % NPAIR == 0 and u >= NPAIR:
                        diag_exp(u // NPAIR - 1)
                    if i in (6, 8, 10):
                        extra(u, (i - 6) // 2)
            act.wait_ge(s_abs, 1)
            sc_.activation(xrow[:, :, C_W:C_H], lg[:], ACT.Gelu).then_inc(s_gelu, 1)

            def z_copy(k):
                act.wait_ge(s_zp, k + 1)
                if k >= 3:
                    act.wait_ge(s_y, k - 2)
                zp = S[0][:, 512 * (k % 2):512 * (k % 2) + 512]
                ep = S[1][0:32, 512 * (k % 2):512 * (k % 2) + P]
                sc_.copy(zT[:, k % 3, :], zp)
                sc_.copy(eT[:, k % 3, :], ep).then_inc(s_zc, 1)

            for k in range(ST_TILES):
                z_copy(k)
            act.wait_ge(s_goff, 1)
            groups = act.value_load(nact[0:1, 0:1], min_val=0, max_val=OVG)
            for k in range(ST_TILES, F_TILES):
                with act.If(groups > 4 * (k - ST_TILES)):
                    z_copy(k)

        @block.vector
        def _(dve):
            v = nc.vector
            link = chain(dve, vs)

            def signs(b):
                dve.wait_ge(s_xin[b], 16)
                v.tensor_scalar(sgn[:, b * XB:(b + 1) * XB, :], xin[:, b * XB:(b + 1) * XB, :], 0.0, 0.5,
                                ALU.is_ge, ALU.subtract).then_inc(s_sgn, 1)

            signs(0)
            dve.wait_ge(s_par, 16 * 6)
            v.tensor_scalar(kq[:], kk[:], 0.0, 0.5, ALU.is_ge, ALU.subtract).then_inc(s_kq, 1)
            signs(1)
            for b in range(B):
                bt = slice(b * NT, (b + 1) * NT)
                if b + 2 < B:
                    signs(b + 2)
                if b == 0:
                    dve.wait_ge(s_bn, 1)
                dve.wait_ge(s_cv, b + 1)
                hv = xrow[:, bt, C_H:C_ID]
                cv = S[1][:, 512 * (b % 2):512 * (b % 2) + NT * D].rearrange("p (t d) -> p t d", t=NT)
                if b == 0:
                    dve.wait_ge(s_fill, 16)
                v.tensor_tensor(hv, cv, bnA[:].unsqueeze(1).to_broadcast([P, NT, D]), ALU.mult).then_inc(s_h, 1)
                dve.wait_ge(s_h, b + 1)
                link(v.tensor_tensor(hv, hv, bnC[:].unsqueeze(1).to_broadcast([P, NT, D]), ALU.add))
                link(v.tensor_reduce(ln1[:, 0, :], hv, X, ALU.add))
                link(v.tensor_scalar(ln1[:, 0, :], ln1[:, 0, :], -1.0 / D, None, ALU.mult))
                link(v.tensor_tensor(cent[:], hv, ln1[:, 0, :].unsqueeze(2).to_broadcast([P, NT, D]), ALU.add))
                if b >= 1:
                    dve.wait_ge(s_xhl, b)
                link(v.tensor_tensor(sq[:], cent[:], cent[:], ALU.mult))
                v.tensor_reduce(ln1[:, 1, :], sq[:], X, ALU.add).then_inc(s_sum, 1)
                dve.wait_ge(s_rs, b + 1)
                v.tensor_tensor(sq[:], cent[:], ln1[:, 3, :].unsqueeze(2).to_broadcast([P, NT, D]),
                                ALU.mult).then_inc(s_xn, 1)
                if b == 0:
                    dve.wait_ge(s_w, 32)
                    for g in range(3):
                        gs = slice(g * H * D, (g + 1) * H * D)
                        src = wst[:, gs].rearrange("p (d h) -> p h d", h=H)
                        hi = wq[:, 0, gs].rearrange("p (h d) -> p h d", h=H)
                        lo = wq[:, 1, gs].rearrange("p (h d) -> p h d", h=H)
                        link(v.tensor_copy(hi, src))
                        last = v.tensor_tensor(lo, src, hi, ALU.subtract)
                    last.then_inc(s_wq, 1)
                    dve.wait_ge(s_bq, 32)
                    for a in range(2):
                        hs = slice(a * D, (a + 1) * D)
                        ins = v.tensor_copy(bq[hs, :].rearrange("p (g j) -> p g j", g=3), bqn[hs, :, a::2])
                    link(ins)
                    v.tensor_scalar(bq8[:], bq[:], D ** -0.5, None, ALU.mult).then_inc(s_bn, 1)

            def hi_cast(kind, w):
                n = "qk".index(kind)
                dve.wait_ge(s_ue, unit_no[(kind, w, 0)] + 1)
                if w >= 2:
                    dve.wait_ge(s_st[(w - 2) % 3], 16 * 8 * ((w - 2) // 3 + 1))
                v.tensor_copy(hl[:, w % 2, n, 0, 0:QN], (q32, k32)[n][:, w % 2, 0:QN]).then_inc((s_qc, s_kc)[n], 1)

            def maxima(u, i):
                n = 2 * NT * u + i
                b, j = divmod(u, NPAIR)
                dve.wait_ge(s_score, n + 1)
                v.tensor_reduce(nm[:, b % 2, j, i:i + 1], S[n % 3][:, 0:N], X, ALU.max, negate=True).then_inc(s_max, 1)

            def diag_weights(b):
                dve.wait_ge(s_exp, 2 * NT * NPAIR * (b + 1))
                dve.wait_ge(s_ue, diag_unit(NPAIR * b + NPAIR - 1) + 1)
                v.reciprocal(sm[:, b % 2], sm[:, b % 2])
                v.tensor_tensor(at[:, b % 2], dg[:, b % 2], nm[:, b % 2], ALU.add).then_inc(s_ex1, 1)

            def diag_scale(b):
                dve.wait_ge(s_ex2, b + 1)
                link(v.tensor_tensor(at[:, b % 2], at[:, b % 2], sm[:, b % 2], ALU.mult))
                if b >= 1:
                    dve.wait_ge(s_uf, unit_no[("bc", b - 1, NPAIR - 1)] + 1)
                link(v.tensor_copy(ath[:, 0], at[:, b % 2]))
                v.tensor_tensor(ath[:, 1], at[:, b % 2], ath[:, 0], ALU.subtract).then_inc(s_at, 1)

            def extra(u, n):
                es = extras(u)
                if n >= len(es) or es[n] is None:
                    return
                kind, b, k = es[n]
                bt = slice(b * NT, (b + 1) * NT)
                if kind == "bc":
                    dve.wait_ge(s_uf, unit_no[("bc", b, k)] + 1)
                    if b >= 1 and k == 0:
                        dve.wait_ge(s_uf, unit_no[("o", b - 1, 0)] + 1)
                    c = START[-1]
                    e = (NT - 1) * P
                    vt = vT[:, (NPAIR * b + k) % 8, :]
                    v.tensor_tensor(avT[:, k, 0:e], vt[:, 0:e], U[:, 0:e], ALU.mult)
                    v.tensor_tensor(avT[:, k, e:], vt[:, c:N], U[:, e:NT * P], ALU.mult).then_inc(s_av, 1)
                    dve.wait_ge(s_av, NPAIR * b + k + 1)
                    dve.sem_inc(s_ue, 1)
                elif kind == "o":
                    dve.wait_ge(s_uf, unit_no[("o", b, 0)] + 1)
                    dve.wait_ge(s_hb, b + 1)
                    hv = xrow[:, bt, C_H:C_ID]
                    v.tensor_tensor(hv, U[:, 0:NT * D].rearrange("p (t d) -> p t d", t=NT), hv,
                                    ALU.add).then_inc(s_ue, 1)
                    dve.wait_ge(s_ue, unit_no[("o", b, 0)] + 1)
                    v.tensor_reduce(ln2[:, 0, :], hv, X, ALU.add).then_inc(s_h2, 1)
                elif kind == "r":
                    dve.wait_ge(s_uf, unit_no[("r", b, 0)] + 1)
                    rm = ML[:, :, 0:LEAVES]
                    v.tensor_tensor(rm, U[:, 0:NT * P].rearrange("p (t n) -> p t n", t=NT), m7[:, bt, :],
                                    ALU.mult).then_inc(s_ue, 1)
                    dve.wait_ge(s_ue, unit_no[("r", b, 0)] + 1)
                    v.tensor_reduce(rank[:, bt], rm, X, ALU.add).then_inc(s_rk, 1)

            def ln2_sumsq(b):
                dve.wait_ge(s_c2, b + 1)
                v.tensor_reduce(ln2[:, 1, :], sq[:], X, ALU.add).then_inc(s_ss2, 1)

            def path_logits(b):
                dve.wait_ge(s_ml, b + 1)
                for lv in range(DEPTH):
                    n = 2 ** lv
                    last = v.tensor_reduce(lg[:, b * NT:(b + 1) * NT, lv], ML[:, :, n - 1:2 * n - 1], X, ALU.add)
                last.then_inc(s_lg, 1)
                dve.wait_ge(s_lg, b + 1)

            for w in range(AHEAD):
                hi_cast("q", w)
                hi_cast("k", w)
            for u in range(NU + NPAIR):
                b, ph = u // NPAIR - 1, u % NPAIR
                for i in range(2 * NT):
                    if u < NU:
                        maxima(u, i)
                    if b >= 0 and ph == 0 and i == 1:
                        diag_weights(b)
                    if b >= 0 and ph == 0 and i == 4:
                        diag_scale(b)
                    if i in (3, 5) and u + AHEAD < NU:
                        hi_cast("qk"[(i - 3) // 2], u + AHEAD)
                    if i in (6, 8, 10):
                        if b >= 0 and ph == 3 and i == 10:
                            if b == B - 1:
                                routing(b, dve, v, link)
                            path_logits(b)
                        extra(u, (i - 6) // 2)
                    if b >= 0 and ph == 1 and i == 11:
                        ln2_sumsq(b)

            lgb = sq[:].rearrange("p t d -> p (t d)")[:, 0:TT * (DEPTH - 1)].rearrange("p (t l) -> p t l", t=TT)
            dve.wait_ge(s_lg, B)
            dve.wait_ge(s_ss2, B)
            link(v.tensor_scalar(lgb, lg[:, :, 0:DEPTH - 1], 0.0, None, ALU.is_gt))
            link(v.tensor_tensor(lgb, lgb, pw2[:].unsqueeze(1).to_broadcast([P, TT, DEPTH - 1]), ALU.mult))
            link(v.tensor_reduce(leaf[:], lgb, X, ALU.add))
            v.scalar_tensor_tensor(lg[:], lg[:], -1.0, lg[:], ALU.mult, ALU.max).then_inc(s_abs, 1)
            dve.wait_ge(s_cnt, 1)
            link(v.tensor_scalar(ogi[:, 0:1], U[:, 0:1], -1.0, float(G - 1), ALU.add, ALU.max))
            link(v.tensor_scalar(ogi[:, 1:2], ogi[:, 0:1], 5, None, ALU.arith_shift_right))
            v.tensor_copy(og[:], ogi[:, 1:2]).then_inc(s_og, 1)
            dve.wait_ge(s_pre, 1)
            v.tensor_copy(ovb[:], U[:, 128:256])
            link(v.tensor_copy(endg[:, 0:1], U[:, 256:257]))
            v.tensor_scalar(ind[:], giota[:], endg[:, 0:1], None, ALU.is_ge).then_inc(s_ind, 1)
            om = lm[:].rearrange("p a t n -> p (a t n)")[:, 0:TT * LEAVES // 2].bitcast(bf16).rearrange(
                "p (t n) -> p t n", t=TT)
            link(v.tensor_tensor(om, m7[:], ovb[:].unsqueeze(1).to_broadcast([P, TT, LEAVES]), ALU.mult))
            n = LEAVES // 2
            while n >= 16:
                link(v.tensor_tensor(om[:, :, 0:n], om[:, :, 0:n], om[:, :, n:2 * n], ALU.add))
                n //= 2
            link(v.tensor_reduce(sc[:, 0, :], om[:, :, 0:2 * n], X, ALU.add))
            link(v.tensor_scalar(sc[:, 0, :], sc[:, 0, :], float(G), float(STAT - G), ALU.mult, ALU.add))
            link(v.tensor_scalar(leaf[:], leaf[:], float(G), None, ALU.mult))
            link(v.tensor_tensor(sc[:, 0, :], sc[:, 0, :], leaf[:], ALU.subtract))
            link(v.tensor_scalar(sc[:, 1, :], rank[:], float(G), None, ALU.is_ge))
            link(v.tensor_tensor(sc[:, 0, :], sc[:, 0, :], sc[:, 1, :], ALU.mult))
            link(v.tensor_tensor(sc[:, 1, :], leaf[:], rank[:], ALU.add))
            link(v.tensor_tensor(sc[:, 2, :], sc[:, 0, :], sc[:, 1, :], ALU.add))
            link(v.tensor_scalar(sc[:, 3, 0:1], valid[:, NT - 1:NT], -float(BIG), float(BIG), ALU.mult, ALU.add))
            dup = sc[:, 2, :].rearrange("p (b t) -> p b t", b=B)[:, :, NT - 1]
            link(v.tensor_scalar(dup, dup, sc[:, 3, 0:1], None, ALU.add))
            v.tensor_copy(slot[:], sc[:, 2, :]).then_inc(s_slot, 1)
            dve.wait_ge(s_lam, 1)
            link(v.tensor_scalar(act_f[:, 0:OVG], U[0:1, 512:512 + OVG], float(LEAVES), None, ALU.is_lt))
            link(v.tensor_reduce(act_f[:, OVG:OVG + 1], act_f[:, 0:OVG], X, ALU.add))
            v.tensor_copy(nact[:], act_f[:, OVG:OVG + 1])
            link(v.tensor_scalar(lamp[:], U[0:32, 512:512 + OVG], float(LEAVES - 1), None, ALU.min))
            v.tensor_copy(lami[:], lamp[0:1, :])
            lk = lamp[:].rearrange("p (k g) -> p k g", g=4)
            link(v.tensor_scalar(shift[:], shift[:], DEPTH - 1, None, ALU.bitwise_and))
            link(v.tensor_scalar(shift[:], shift[:], -1.0, float(DEPTH - 1), ALU.mult, ALU.add))
            link(v.tensor_tensor(lk, lk, gmaskp[:].unsqueeze(1).to_broadcast([32, OV_TILES, 4]), ALU.mult))
            link(v.tensor_reduce(endg[0:32, 0:OV_TILES], lk, X, ALU.add))
            link(v.tensor_scalar(oidx[:, 1, :], endg[0:32, 0:OV_TILES], float(LEAVES), None, ALU.add))
            link(v.tensor_tensor(oidx[:, 1, :], oidx[:, 1, :], shift[:], ALU.arith_shift_right))
            v.tensor_scalar(oidx[:, 0, :], oidx[:, 1, :], -1.0, None, ALU.add).then_inc(s_goff, 1)

            def make_z(k):
                if k % 4 == 0:
                    dve.wait_ge(s_xsr[k // 4 % NX], 16 * (k // 4 // NX + 1))
                if k >= 3:
                    dve.wait_ge(s_zp, k - 2)
                xk = xs[:, (k // 4) % NX, k % 4, :]
                wk = xk[:, C_W:C_H]
                v.tensor_tensor(z[:, k % 3, 0:DEPTH * D].rearrange("p (l d) -> p l d", l=DEPTH),
                                xk[:, 0:D].unsqueeze(1).to_broadcast([P, DEPTH, D]),
                                wk.unsqueeze(2).to_broadcast([P, DEPTH, D]), ALU.mult)
                v.tensor_tensor(z[:, k % 3, DEPTH * D:ZW].rearrange("p (g l) -> p g l", g=4),
                                wk.unsqueeze(1).to_broadcast([P, 4, DEPTH]),
                                gmask[:].unsqueeze(2).to_broadcast([P, 4, DEPTH]), ALU.mult).then_inc(s_z, 1)

            def tile_out(k):
                dve.wait_ge(s_y, k + 1)
                if k >= NO:
                    dve.wait_ge(s_outr[k % NO], 16 * (k // NO))
                xk = xs[:, (k // 4) % NX, k % 4, C_H:C_ID]
                o, y = yo[:, k % NO, :], y_bank(k)
                if k < ST_TILES:
                    v.tensor_tensor(o, y[:, 0:D], xk, ALU.add).then_inc(s_yo, 1)
                else:
                    link(v.tensor_tensor(o, y[:, 4 * D:5 * D], xk, ALU.add))
                    for g in range(4):
                        gs = slice(g * G, (g + 1) * G)
                        last = v.tensor_tensor(o[gs, :], y[0:G, g * D:(g + 1) * D], o[gs, :], ALU.add)
                    last.then_inc(s_yo, 1)

            dve.wait_ge(s_goff, 1)
            groups = dve.value_load(nact[0:1, 0:1], min_val=0, max_val=OVG)
            make_z(0)
            make_z(1)
            for k in range(F_TILES):
                if k + 2 < ST_TILES:
                    make_z(k + 2)
                elif k + 2 < F_TILES:
                    with dve.If(groups > 4 * (k + 2 - ST_TILES)):
                        make_z(k + 2)
                if k < ST_TILES:
                    tile_out(k)
                else:
                    with dve.If(groups > 4 * (k - ST_TILES)):
                        tile_out(k)


_INS = ["x", "L0_tok_kernel", "L0_tok_bias", "L0_tok_beta", "L0_tok_moving_mean", "L0_tok_moving_var",
        "L0_attn_Wqkv", "L0_attn_bqkv", "L0_attn_W0", "L0_attn_b0", "L0_ffn_w1s", "L0_ffn_b1s",
        "L0_ffn_w2s", "L0_ffn_b2s"]


def kernel(**inputs):
    import concourse.bacc as _bacc
    from concourse import mybir as _mybir
    from concourse.bass_utils import run_bass_kernel_spmd as _run

    nc = _bacc.Bacc("TRN2", target_bir_lowering=False, num_devices=1)
    arrays, args = {}, []
    for name in _INS:
        a = np.ascontiguousarray(inputs[name])
        arrays[f"in_{name}"] = a
        args.append(nc.dram_tensor(f"in_{name}", a.shape, _mybir.dt.from_np(a.dtype), kind="ExternalInput").ap())
    rows = nc.dram_tensor("sorted_rows", (SLOTS, RW), _mybir.dt.float32).ap()
    out = nc.dram_tensor("out_0", (B, N, D), _mybir.dt.float32, kind="ExternalOutput").ap()
    tower(nc, *args, rows, out)
    r = _run(nc, [arrays], core_ids=[0])
    return r.results[0]["out_0"]
```

```python
from contextlib import ExitStack

import numpy as np
import concourse.bass as bass
from concourse import mybir

B, NIN, CIN = 4, 750, 128
TAPS, D = 3, 64
N = NIN - TAPS + 1
H = 8
NPAIR = H // 2
DEPTH = 8
NODES = 2 ** DEPTH - 1
LEAVES = 2 ** (DEPTH - 1)
P = 128
NT = -(-N // P)
START = [min(t * P, N - P) for t in range(NT)]
DUP = NT * P - N
TT = B * NT
XP = 125
XB = NIN // XP
T = B * N
NP3 = 250
QN = 3 * NP3
PAD = QN + 2
XW = T + 2
G = 32
OVG = 96
STAT = LEAVES * G
SLOTS = STAT + OVG * G
ST_TILES, OV_TILES = STAT // P, OVG * G // P
F_TILES = ST_TILES + OV_TILES
C_ONE, C_W, C_H, C_ID = D, D + 1, D + 1 + DEPTH, 2 * D + 1 + DEPTH
RW = C_ID + 1
BIG = 1 << 20
LN_EPS, BN_EPS = 1e-5, 1e-3
T03, T45 = 0, 4 * 2 ** 3
T6 = T45 + 2 * 2 ** 5
LOWN = T6 + 2 ** 6 + 2
LOW = ((T03, (0, 1, 2, 3)), (T45, (4, 5)), (T6, (6,)))


def tower(nc, x, k_tok, bias, beta, mean, var, Wqkv, bqkv, W0, b0, w1s, b1s, w2s, b2s, rows, out):
    f32, f16, bf16, i32, u32 = (mybir.dt.float32, mybir.dt.float16, mybir.dt.bfloat16,
                                mybir.dt.int32, mybir.dt.uint32)
    ALU = mybir.AluOpType
    ACT = mybir.ActivationFunctionType
    X = mybir.AxisListType.X
    ctx = ExitStack()
    with ctx:
        def sb(name, shape, dt=f32):
            return ctx.enter_context(nc.sbuf_tensor(name, shape, dt))

        def sem(name):
            return ctx.enter_context(nc.semaphore(name))

        w7all = sb("w7", [P, (LEAVES + 1) * D])
        w7 = w7all[:, 0:LEAVES * D]
        pool_a = sb("pool_a", [P, max(13 * PAD, LOWN * D)])
        st = pool_a[:, 0:6 * 3 * PAD // 2].bitcast(f16).rearrange("p (r a h n) -> p r a h n", r=3, a=3, h=2)
        qst, kst = st[:, :, 0], st[:, :, 1:3]
        hl0 = 6 * 3 * PAD // 2
        hl = pool_a[:, hl0:hl0 + 4 * PAD].bitcast(f16).rearrange("p (r k s n) -> p r k s n", r=2, k=2, s=2)
        wlow = pool_a[:, 0:LOWN * D]
        xhT = sb("xhT", [P, XW], f16)
        wq = sb("wq", [P, 2, 3 * H * D], f16)
        q32 = sb("q32", [P, 2, PAD])
        k32 = sb("k32", [P, 2, PAD])
        qk = sb("qk", [P, NT * P])
        vT = sb("vT", [P, 8, PAD])
        avT = sb("avT", [P, NPAIR, NT * P])
        xrow = sb("xrow", [P, TT, RW])
        xT2 = sb("xT2", [D + 1, NT * P])
        lm = sb("lm", [P, 2, NT, 256])
        L, M = lm[:, 0], lm[:, 1]
        ML = sb("ML", [P, NT, 256])
        gt = sb("gt", [P, NT, LEAVES])
        m7 = sb("m7", [P, TT, LEAVES], bf16)
        run = sb("run", [P, NT + 1, LEAVES], bf16)
        xin = lm[0:XP].rearrange("p a t n -> p (a t n)")[:, 0:B * XB * CIN].rearrange(
            "p (j c) -> p j c", c=CIN)
        sgn = avT[0:XP].rearrange("p j n -> p (j n)")[:, 0:B * XB * CIN // 2].bitcast(bf16).rearrange(
            "p (j c) -> p j c", c=CIN)
        wst = vT[:].rearrange("p j n -> p (j n)")[:, 0:3 * H * D]
        xT = ML[:].rearrange("p t n -> p (t n)")[:, 0:NIN].bitcast(bf16).rearrange("p (r n) -> p r n", r=2)
        cent = sb("cent", [P, 2, NT, D])
        xn = sb("xn", [P, NT, D])
        sq = sb("sq", [P, NT, D])
        xhl = sb("xhl", [P, NT, 2, D], f16)
        kk = sb("kk", [P, TAPS, D])
        kq = sb("kq", [P, TAPS, D], bf16)
        zrow = sb("zrow", [P, RW])
        par = sb("par", [D, 4])
        b0r = sb("b0r", [P, D])
        bnp = sb("bnp", [D, 3])
        bn = sb("bn", [P, 2, D])
        half = sb("half", [P, D])
        bqn = sb("bqn", [P, 3, H])
        bq = sb("bq", [P, 12])
        bq8 = sb("bq8", [P, 12])
        w0p = sb("w0p", [P, NPAIR, D])
        w1n = sb("w1n", [P, 2, D])
        w1T = sb("w1T", [D + 1, 256])
        idf = sb("idf", [P, P])
        idb = sb("idb", [P, P], bf16)
        idh = sb("idh", [P, P], f16)
        tri = sb("tri", [P, P], bf16)
        tri_i = sb("tri_i", [P, P], bf16)
        ones = sb("ones", [P, P], bf16)
        sel = sb("sel", [P, 2])
        valid = sb("valid", [P, NT])
        nm = sb("nm", [P, 2, NPAIR, 2 * NT])
        sm = sb("sm", [P, 2, NPAIR, 2 * NT])
        dg = sb("dg", [P, 2, NPAIR, 2 * NT])
        at = sb("at", [P, 2, NPAIR, 2 * NT])
        ath = sb("ath", [P, 2, NPAIR, 2 * NT], f16)
        ln1 = sb("ln1", [P, 2, 4, NT])
        ln2 = sb("ln2", [P, 4, NT])
        lg = sb("lg", [P, TT, DEPTH])
        rank = sb("rank", [P, TT])
        leaf = sb("leaf", [P, TT])
        sc = sb("sc", [P, 4, TT])
        slot = sb("slot", [P, TT], i32)
        oslot = sb("oslot", [P, TT], i32)
        lgb = sb("lgb", [P, NT, DEPTH - 1])
        dup_out = sb("dup_out", [P, 1])
        pw2 = sb("pw2", [P, DEPTH - 1])
        ogi = sb("ogi", [P, 2], i32)
        og = sb("og", [P, 1], bf16)
        endg = sb("endg", [P, 1])
        ovb = sb("ovb", [P, LEAVES], bf16)
        giota = sb("giota", [P, OVG])
        ind = sb("ind", [P, OVG], bf16)
        warm = sb("warm", [1, 1])
        lamf = sb("lamf", [1, OVG])
        lami = sb("lami", [1, OVG // 2], i32)
        act_f = sb("act_f", [1, OVG + 1])
        nact = sb("nact", [1, 1], i32)
        NX = 6
        xs = vT[:].rearrange("p j n -> p (j n)")[:, 0:NX * 4 * RW].rearrange("p (r t c) -> p r t c", r=NX, t=4)
        z0 = NX * 4 * RW
        wy = vT[:].rearrange("p j n -> p (j n)")[:, z0:z0 + 2 * DEPTH * D].rearrange("p (r c) -> p r c", r=2)
        yv = vT[:].rearrange("p j n -> p (j n)")[:, z0 + 2 * DEPTH * D:z0 + 4 * DEPTH * D].rearrange(
            "p (r c) -> p r c", r=2)
        xsT = avT[:].rearrange("p j n -> p (j n)")[:, 0:3 * 512].rearrange("p (r c) -> p r c", r=3)
        NO = 12
        yo = lm[:].rearrange("p a t n -> p (a t n)")[:, 0:NO * D].rearrange("p (r c) -> p r c", r=NO)

        S = [ctx.enter_context(nc.psum_tensor(f"S{i}", [P, 1024], f32)) for i in range(3)]
        U = ctx.enter_context(nc.psum_tensor("U", [P, 1024], f32))
        U_D = 1000

        NY = 6

        def y_bank(n):
            return ([S[1], S[2], U][n // 2 % 3])[:, 512 * (n % 2):512 * (n % 2) + 512]

        def banks(k):
            return k + 3 * max(0, k - ST_TILES)

        (s_par, s_w, s_bq, s_w0, s_w1, s_b1, s_tab, s_low, s_fill, s_id, s_segs, s_sego) = [
            sem(n) for n in ("params_in", "wqkv_in", "bq_in", "w0_in", "w1_in",
                             "b1_in", "table_in", "low_table_in", "rows_filled", "consts_ready", "own_slots_written",
                             "overflow_written")]
        (s_sgn, s_xtp, s_xtc, s_cv, s_h, s_sum, s_rs, s_xn, s_hi, s_xhl, s_xhp, s_xhT, s_wq, s_bnb, s_kq, s_w1p,
         s_w1c, s_hb) = [sem(n) for n in (
            "signs", "x_blocks_T", "x_blocks_copied", "conv_done", "h_ready", "ln_sums", "ln_rstd", "ln_x",
            "x_hi", "x_lo", "xhat_T", "xhat_copied", "wq_split", "bn_rows", "kq_ready", "w1_T", "w1_copied",
            "h_plus_b0")]
        (s_uf, s_ue, s_score, s_max, s_exp, s_qc, s_kc, s_lo, s_prod, s_av) = [sem(n) for n in (
            "unit_filled", "unit_emptied", "scores", "maxima", "exps", "qk_hi_q", "qk_hi_k", "qk_lo", "qk_prod",
            "av_ready")]
        s_xin = [sem(f"x_in{b}") for b in range(B)]
        s_xsr = [sem(f"rows_in{r}") for r in range(NX)]
        s_outr = [sem(f"out_written{r}") for r in range(NO)]
        s_st = [sem(f"stacks_in{r}") for r in range(3)]
        (s_ex1, s_ex2, s_at, s_h2, s_c2, s_ss2, s_xh2, s_ml, s_lg, s_m7, s_rk, s_gelu) = [sem(n) for n in (
            "diag_shifted", "diag_exp", "at_ready", "h2_ready", "ln2_squares", "ln2_sumsq", "xhat2_ready",
            "masked_logits", "path_logits", "leaf_masks", "ranks", "gelu_done")]
        (s_cnt, s_og, s_pre, s_ind, s_lam, s_goff, s_slot, s_oslot, s_rs2) = [sem(n) for n in (
            "leaf_counts", "leaf_groups", "group_prefix", "group_index", "group_leaf", "group_offsets", "slots",
            "overflow_slots", "ln2_rstd")]
        (s_b0, s_bnp, s_bn, s_bq8, s_z7, s_zl, s_xp, s_xc, s_y, s_yv, s_wy, s_sl, s_yo) = [sem(n) for n in (
            "b0_in", "bn_by_feature", "bn_ready", "q_bias_ready", "w7_zeros", "low_zeros", "xs_T", "xsT_copied", "y_ready", "y_moved", "weighted", "levels_summed", "rows_out")]
        vs, ps_, as_ = sem("vector_step"), sem("pool_step"), sem("scalar_step")

        def chain(engine, s):
            n = [0]

            def link(ins):
                n[0] += 1
                ins.then_inc(s, 1)
                engine.wait_ge(s, n[0])
            return link

        def extras(u):
            b, ph = u // NPAIR - 1, u % NPAIR
            if b < 0:
                return []
            return [[("bc", b, 0), ("bc", b, 1), ("bc", b, 2)], [("bc", b, 3), ("o", b, 0), ("o", b, 1)],
                    [("t", b, 0), ("l", b, 0), ("l", b, 1)] if b < B - 1 else
                    [("t", b, 0), ("r", b - 1, 0), ("l", b, 0)],
                    [("r", b - 1, 0) if b else None, None, None] if b < B - 1 else
                    [("l", b, 1), None, ("r", b, 0)]][ph]

        NU = B * NPAIR
        AHEAD = 2
        units = [(k, w, 0) for w in range(AHEAD) for k in "qkv"]
        for u in range(NU + NPAIR):
            if u < NU and u + AHEAD < NU:
                units += [(k, u + AHEAD, 0) for k in "qkv"]
            if u + AHEAD == NU:
                units.append(("d", NU - 1, 0))
            units += [e for e in extras(u) if e]
        unit_no = {k: n for n, k in enumerate(units)}

        def bc_banks(b, j):
            return S[0] if b == B - 1 and j % 2 else U

        def diag_unit(w):
            return unit_no[("v", w + 1, 0) if w + 1 < NU else ("d", w, 0)]

        def path_masks(b, eng, ops, link):
            eng.wait_ge(s_ue, unit_no[("l", b, 1)] + 1)
            if b >= 1:
                eng.wait_ge(s_rk, b)
            link(ops.memset(M[:, :, 0:1], 1.0))
            link(ops.tensor_scalar(gt[:, :, 0:LEAVES - 1], L[:, :, 0:LEAVES - 1], 0.0, None, ALU.is_gt))
            for lv in range(DEPTH - 1):
                n = 2 ** lv
                par_ = M[:, :, n - 1:2 * n - 1]
                kid = M[:, :, 2 * n - 1:4 * n - 1].rearrange("p t (n c) -> p t n c", c=2)
                link(ops.tensor_tensor(kid[:, :, :, 1], par_, gt[:, :, n - 1:2 * n - 1], ALU.mult))
                link(ops.tensor_tensor(kid[:, :, :, 0], par_, kid[:, :, :, 1], ALU.subtract))

        def leaf_masks(b, eng, ops, link):
            if b >= 1:
                eng.wait_ge(s_lg, b)
            ops.tensor_tensor(ML[:, :, 0:NODES], M[:, :, 0:NODES], L[:, :, 0:NODES], ALU.mult).then_inc(s_ml, 1)
            t0 = b * NT
            link(ops.tensor_tensor(m7[:, t0:t0 + NT, :], M[:, :, LEAVES - 1:NODES],
                                   valid[:].unsqueeze(2).to_broadcast([P, NT, LEAVES]), ALU.mult))
            if b >= 1:
                link(ops.tensor_tensor(run[:, 0, :], run[:, NT, :], ones[:], ALU.mult))
            for j in range(NT):
                link(ops.tensor_tensor(run[:, j + 1, :], run[:, j, :], m7[:, t0 + j, :], ALU.add))
            eng.sem_inc(s_m7, 1)

        block = ctx.enter_context(nc.Block())

        @block.sync
        def _(sp):
            xv = x.rearrange("b (j p) c -> p (b j) c", p=XP)
            for b in range(B):
                sp.dma_start(xin[:, b * XB:(b + 1) * XB, :], xv[:, b * XB:(b + 1) * XB, :]).then_inc(s_xin[b], 16)
                if b == 0:
                    sp.dma_start(kk[:], k_tok.rearrange("t c o -> c t o")).then_inc(s_par, 16)
                    for n, v in enumerate((bias, beta, mean, var)):
                        sp.dma_start(par[:, n:n + 1], v.unsqueeze(1)).then_inc(s_par, 16)
            sp.dma_start(wst[0:D, :], Wqkv).then_inc(s_w, 16)
            sp.dma_start(wst[D:P, :], Wqkv).then_inc(s_w, 16)
            for a in range(2):
                sp.dma_start(bqn[a * D:(a + 1) * D], bqkv.rearrange("(g d h) -> d g h", g=3, d=D)).then_inc(s_bq, 16)
            sp.dma_start(b0r[:], b0.partition_broadcast(P)).then_inc(s_b0, 16)
            w0v = W0.rearrange("(d j a) o -> a d j o", j=NPAIR, a=2)
            for a in range(2):
                sp.dma_start(w0p[a * D:(a + 1) * D, :, :], w0v[a]).then_inc(s_w0, 16)
            sp.dma_start(w1n[:, 0, :], w1s[0:P, :]).then_inc(s_w1, 16)
            sp.dma_start(w1n[0:NODES - P, 1, :], w1s[P:NODES, :]).then_inc(s_w1, 16)
            sp.dma_start(w1T[D:D + 1, 0:NODES], b1s.unsqueeze(0)).then_inc(s_b1, 16)
            wv = w2s.rearrange("n d o -> d n o")
            for w in range(NU):
                r, c = w % 3, w % 2
                sp.wait_ge(s_lo, 2 * w + 2)
                if w >= 3:
                    sp.wait_ge(s_score, 2 * NT * (w - 2))
                for a in range(2):
                    src = slice(a * D, (a + 1) * D)
                    for half_ in range(2):
                        dst = slice(half_ * D, (half_ + 1) * D)
                        sp.dma_start(qst[dst, r, a, 0:QN], hl[src, c, 0, half_, 0:QN]).then_inc(s_st[r], 16)
                        sp.dma_start(kst[dst, r, :, a, 0:QN], hl[src, c, 1, :, 0:QN]).then_inc(s_st[r], 16)
                if w == 1:
                    sp.wait_ge(s_id, 2)
                    sp.dma_start(rows.rearrange("(t p) c -> p t c", p=P),
                                 zrow[:].unsqueeze(1).to_broadcast([P, F_TILES, RW])).then_inc(s_fill, 16)
                if w == 4:
                    sp.dma_start(w7[0:D, :].rearrange("p (n o) -> p n o", o=D),
                                 wv[:, LEAVES - 1:, :]).then_inc(s_tab, 16)
                    sp.wait_ge(s_z7, 1)
                    sp.dma_start(w7[D:D + 1, :].rearrange("p (n o) -> p n o", o=D),
                                 b2s[LEAVES - 1:, :].unsqueeze(0)).then_inc(s_tab, 16)
            sp.wait_ge(s_score, 2 * NT * NU)
            tv = wlow.rearrange("p (e o) -> p e o", o=D)
            bv = b2s.unsqueeze(0)
            for rows_, src in ((slice(0, D), wv), (slice(D, D + 1), bv)):
                if src is bv:
                    sp.wait_ge(s_zl, 1)
                for e0, lvs in LOW:
                    m = 2 ** lvs[-1]
                    dst = tv[rows_, e0:e0 + m * len(lvs), :].rearrange("p (m s) o -> p m s o", s=len(lvs))
                    for i, lv in enumerate(lvs):
                        n = 2 ** lv
                        for r in range(m // n):
                            sp.dma_start(dst[:, r::m // n, i, :], src[:, n - 1:2 * n - 1, :]).then_inc(s_low, 16)
            rv = rows.rearrange("(t p) c -> p t c", p=P)
            sp.wait_ge(s_segs, 16 * TT)
            def load_rows(k):
                if k >= NX:
                    for t in range(4 * (k - NX), 4 * (k - NX) + 4):
                        sp.wait_ge(s_outr[t % NO], 16 * (t // NO + 1))
                sp.dma_start(xs[:, k % NX], rv[:, 4 * k:4 * k + 4, :]).then_inc(s_xsr[k % NX], 16)

            for k in range(ST_TILES // 4):
                load_rows(k)
            sp.wait_ge(s_goff, 1)
            sp.wait_ge(s_sego, 16 * TT)
            groups = sp.value_load(nact[0:1, 0:1], min_val=0, max_val=OVG)
            for k in range(ST_TILES // 4, F_TILES // 4):
                with sp.If(groups > 4 * (4 * k - ST_TILES)):
                    load_rows(k)
            for k in range(ST_TILES - NO, ST_TILES):
                sp.wait_ge(s_outr[k % NO], 16 * (k // NO + 1))
            for m in range(ST_TILES // 4, F_TILES // 4):
                with sp.If(groups > 4 * (4 * m - ST_TILES)):
                    for k in range(4 * m, 4 * m + 4):
                        sp.wait_ge(s_outr[k % NO], 16 * (k // NO + 1))

        @block.gpsimd
        def _(pool):
            gp = nc.gpsimd
            link = chain(pool, ps_)
            gp.memset(half[:], -0.5)
            link(gp.memset(idf[:], 0.0))
            link(gp.affine_select(out=idf[:], in_=idf[:], compare_op=ALU.not_equal, fill=1.0, base=0,
                                  pattern=[[-1, P]], channel_multiplier=1))
            gp.tensor_copy(idb[:], idf[:])
            link(gp.tensor_copy(idh[:], idf[:]))
            pool.sem_inc(s_id, 1)
            pool.wait_ge(s_par, 16 * 5)
            link(gp.tensor_scalar(bnp[:, 0:1], par[:, 3:4], BN_EPS, 1.0, ALU.add, ALU.mult))
            link(gp.tensor_tensor(bnp[:, 2:3], bnp[:, 0:1], half[0:D, 0:1], ALU.pow))
            link(gp.tensor_tensor(bnp[:, 1:2], par[:, 0:1], par[:, 2:3], ALU.subtract))
            link(gp.tensor_tensor(bnp[:, 1:2], bnp[:, 1:2], bnp[:, 2:3], ALU.mult))
            link(gp.tensor_tensor(bnp[:, 1:2], bnp[:, 1:2], par[:, 1:2], ALU.add))
            link(gp.tensor_scalar(bnp[:, 0:1], bnp[:, 2:3], 4.0, 0.0, ALU.mult, ALU.add))
            pool.sem_inc(s_bnp, 1)
            gp.memset(ones[:], 1.0)
            gp.memset(zrow[:], 0.0)
            gp.memset(xhT[:, T:XW], 0.0)
            gp.memset(run[:, 0, :], 0.0)
            gp.memset(sel[:], 0.0)
            gp.memset(valid[:], 1.0)
            link(gp.memset(tri[:], 1.0))
            link(gp.memset(sel[0:D, 0:1], 1.0))
            link(gp.memset(sel[D:P, 1:2], 1.0))
            gp.affine_select(out=valid[:, NT - 1:NT], in_=valid[:, NT - 1:NT], compare_op=ALU.is_ge, fill=0.0,
                             base=-DUP, pattern=[[0, 1]], channel_multiplier=1)
            gp.affine_select(out=tri_i[:], in_=tri[:], compare_op=ALU.is_ge, fill=0.0, base=0,
                             pattern=[[1, P]], channel_multiplier=-1)
            link(gp.affine_select(out=tri[:], in_=tri[:], compare_op=ALU.is_gt, fill=0.0, base=0,
                                  pattern=[[1, P]], channel_multiplier=-1))
            for lv in range(DEPTH - 1):
                gp.memset(pw2[:, lv:lv + 1], float(G * 2 ** (DEPTH - 2 - lv)))
            link(gp.tensor_scalar(dup_out[:], valid[:, NT - 1:NT], -float(BIG), float(BIG), ALU.mult, ALU.add))
            link(gp.memset(zrow[:, C_ID:C_ID + 1].bitcast(i32), BIG))
            link(gp.memset(w1T[D:D + 1, NODES:256], 0.0))
            pool.sem_inc(s_id, 1)

            def rstd1(b):
                pool.wait_ge(s_sum, b + 1)
                link(gp.tensor_scalar(ln1[:, b % 2, 2, :], ln1[:, b % 2, 1, :], 1.0 / D, LN_EPS, ALU.mult, ALU.add))
                gp.tensor_tensor(ln1[:, b % 2, 3, :], ln1[:, b % 2, 2, :], half[:, 0:NT], ALU.pow).then_inc(s_rs, 1)

            rstd1(0)
            for b in range(B):
                bt = slice(b * NT, (b + 1) * NT)
                if b + 1 < B:
                    rstd1(b + 1)
                pool.wait_ge(s_hi, b + 1)
                gp.tensor_tensor(xhl[:, :, 1, :], xn[:], xhl[:, :, 0, :], ALU.subtract).then_inc(s_xhl, 1)
                if b == 0:
                    pool.wait_ge(s_b0, 16)
                gp.tensor_tensor(xrow[:, bt, C_H:C_ID], xrow[:, bt, C_H:C_ID],
                                 b0r[:].unsqueeze(1).to_broadcast([P, NT, D]), ALU.add).then_inc(s_hb, 1)
            pool.wait_ge(s_hb, B)

            def token_numbers():
                for t in range(TT):
                    b, j = divmod(t, NT)
                    gp.iota(xrow[:, t, C_ID:C_ID + 1].bitcast(i32), pattern=[[0, 1]], base=b * N + START[j],
                            channel_multiplier=1)
                gp.iota(giota[:], pattern=[[1, OVG]], base=0, channel_multiplier=0,
                        allow_small_or_imprecise_dtypes=True)
                link(gp.memset(xrow[:, :, C_ONE:C_ONE + 1], 1.0))
                link(gp.memset(w7[D:P, :], 0.0))
                pool.sem_inc(s_z7, 1)

            def qk_lo(w):
                c = w % 2
                for n, (src, s_c) in enumerate(((q32, s_qc), (k32, s_kc))):
                    pool.wait_ge(s_c, w + 1)
                    gp.tensor_tensor(hl[:, c, n, 1, 0:QN], src[:, c, 0:QN], hl[:, c, n, 0, 0:QN],
                                     ALU.subtract).then_inc(s_lo, 1)
                if w >= 1:
                    pool.wait_ge(s_uf, diag_unit(w - 1) + 1)
                gp.tensor_tensor(qk[:, 0:N], q32[:, c, 0:N], k32[:, c, 0:N], ALU.mult).then_inc(s_prod, 1)

            def ln2_squares(b):
                pool.wait_ge(s_h2, b + 1)
                bt = slice(b * NT, (b + 1) * NT)
                link(gp.tensor_scalar(ln2[:, 2, :], ln2[:, 0, :], -1.0 / D, 0.0, ALU.mult, ALU.add))
                link(gp.tensor_tensor(cent[:, 0], xrow[:, bt, C_H:C_ID],
                                      ln2[:, 2, :].unsqueeze(2).to_broadcast([P, NT, D]), ALU.add))
                gp.tensor_tensor(sq[:], cent[:, 0], cent[:, 0], ALU.mult).then_inc(s_c2, 1)

            def ln2_rstd(b):
                pool.wait_ge(s_ss2, b + 1)
                link(gp.tensor_scalar(ln2[:, 2, :], ln2[:, 1, :], 1.0 / D, LN_EPS, ALU.mult, ALU.add))
                link(gp.tensor_tensor(ln2[:, 3, :], ln2[:, 2, :], half[:, 0:NT], ALU.pow))

            def ln2_x(b):
                bt = slice(b * NT, (b + 1) * NT)
                gp.tensor_tensor(xrow[:, bt, 0:D], cent[:, 0],
                                 ln2[:, 3, :].unsqueeze(2).to_broadcast([P, NT, D]), ALU.mult).then_inc(s_xh2, 1)

            def scatter(t, slots, done):
                gp.indirect_dma_start(rows, bass.IndirectOffsetOnAxis(slots[:, t:t + 1].bitcast(u32), 0),
                                      xrow[:, t, :], None, bounds_check=SLOTS - 1,
                                      oob_is_err=False).then_inc(done, 16)

            def own_slots(b):
                if b == 0:
                    pool.wait_ge(s_fill, 16)
                pool.wait_ge(s_slot, b + 1)
                for t in range(b * NT, (b + 1) * NT):
                    scatter(t, slot, s_segs)

            for w in range(AHEAD):
                qk_lo(w)
            token_numbers()
            for u in range(NU + NPAIR):
                b, ph = u // NPAIR - 1, u % NPAIR
                if u + AHEAD < NU:
                    qk_lo(u + AHEAD)
                if 0 <= b < B - 1 and ph == 3:
                    path_masks(b, pool, gp, link)
                if 1 <= b and ph == 0:
                    leaf_masks(b - 1, pool, gp, link)
                if b >= 2 and ph == 0:
                    own_slots(b - 2)
                if 0 <= b < B - 1 and ph == 1:
                    ln2_squares(b)
                    ln2_rstd(b)
                    ln2_x(b)
                if b == B - 1 and ph == 1:
                    ln2_rstd(b)
                    pool.sem_inc(s_rs2, 1)
            pool.wait_ge(s_score, 2 * NT * NU)
            link(gp.memset(wlow[D:P, :], 0.0))
            pool.sem_inc(s_zl, 1)
            pool.wait_ge(s_uf, unit_no[("o", B - 1, 1)] + 1)
            link(gp.memset(xsT[D:P], 0.0))
            pool.sem_inc(s_zl, 1)
            own_slots(B - 2)
            own_slots(B - 1)
            outf = out.rearrange("b n o -> (b n) o")
            pool.wait_ge(s_oslot, 1)
            FIRST = 6
            for t in range(FIRST):
                scatter(t, oslot, s_sego)
            pool.wait_ge(s_goff, 1)
            groups = pool.value_load(nact[0:1, 0:1], min_val=0, max_val=OVG)

            def rows_out(k):
                pool.wait_ge(s_yo, k + 1)
                ids = xs[:, (k // 4) % NX, k % 4, C_ID:C_ID + 1]
                gp.indirect_dma_start(outf, bass.IndirectOffsetOnAxis(ids.bitcast(u32), 0), yo[:, k % NO, :], None,
                                      bounds_check=T - 1, oob_is_err=False).then_inc(s_outr[k % NO], 16)

            for k in range(ST_TILES):
                rows_out(k)
                if FIRST + k < TT:
                    scatter(FIRST + k, oslot, s_sego)
            for m in range(ST_TILES // 4, F_TILES // 4):
                with pool.If(groups > 4 * (4 * m - ST_TILES)):
                    for k in range(4 * m, 4 * m + 4):
                        rows_out(k)

        @block.tensor
        def _(pe):
            mm = nc.tensor.matmul
            pe.wait_ge(s_id, 1)

            def x_blocks(b):
                pe.wait_ge(s_sgn, b + 1)
                if b >= 2:
                    pe.wait_ge(s_xtc, b - 1)
                xp = S[0][:, 512 * (b % 2):512 * (b % 2) + 384].bitcast(bf16).rearrange("p (j n) -> p j n", j=XB)
                for j in range(XB):
                    last = nc.tensor.transpose(xp[:, j, 0:XP], sgn[:, b * XB + j, :], idb[0:XP, 0:XP])
                last.then_inc(s_xtp, 1)

            def conv(b):
                pe.wait_ge(s_xtc, b + 1)
                pe.wait_ge(s_kq, 1)
                if b >= 2:
                    pe.wait_ge(s_h, b - 1)
                for j in range(NT):
                    o = 512 * (b % 2) + j * D
                    for k in range(TAPS):
                        last = mm(S[1][:, o:o + D], xT[:, b % 2, START[j] + k:START[j] + k + P], kq[:, k, :],
                                  start=(k == 0), stop=(k == TAPS - 1))
                last.then_inc(s_cv, 1)

            def xhat_T(b):
                pe.wait_ge(s_xhl, b + 1)
                if b >= 2:
                    pe.wait_ge(s_xhT, b - 1)
                xp = S[2][:, 512 * (b % 2):512 * (b % 2) + 384].bitcast(f16)
                for j in range(NT):
                    last = nc.tensor.transpose(xp[:, j * P:(j + 1) * P], xhl[:, j].rearrange("p a d -> p (a d)"),
                                               idh[:])
                last.then_inc(s_xhp, 1)

            x_blocks(0)
            x_blocks(1)
            conv(0)
            pe.wait_ge(s_bnp, 1)
            for n in range(2):
                last = mm(U[:, 512 + n * D:512 + (n + 1) * D], bnp[:, n:n + 1].to_broadcast([D, P]), idf[0:D, 0:D],
                          start=True, stop=True)
            last.then_inc(s_bnb, 1)
            x_blocks(2)
            conv(1)
            for b in range(B):
                if b + 3 < B:
                    x_blocks(b + 3)
                if b + 2 < B:
                    conv(b + 2)
                xhat_T(b)
            pe.wait_ge(s_w1, 32)
            nc.tensor.transpose(U[0:D, 0:P], w1n[:, 0, :], idf[:])
            nc.tensor.transpose(U[0:D, P:NODES], w1n[0:NODES - P, 1, :],
                                idf[0:NODES - P, 0:NODES - P]).then_inc(s_w1p, 1)

            def fill(unit):
                if unit_no[unit]:
                    pe.wait_ge(s_ue, unit_no[unit])

            def project(kind, w):
                b, j = divmod(w, NPAIR)
                fill((kind, w, 0))
                base = "qkv".index(kind) * T + b * N
                for s in range(3):
                    r0, g = divmod(base + s, 3)
                    for a in range(2):
                        last = mm(U[:, 256 * s:256 * s + NP3], wq[:, a, g * H * D + j * P:g * H * D + (j + 1) * P],
                                  xhT[:, r0:r0 + NP3], start=(a == 0), stop=(a == 1))
                if w >= 1:
                    n = 2 * "qkv".index(kind)
                    last = diagonal(w - 1, range(n, n + 2))
                last.then_inc(s_uf, 1)

            def diagonal(w, tiles):
                pe.wait_ge(s_prod, w + 1)
                for t in tiles:
                    last = mm(U[:, U_D + t:U_D + t + NT + 1:NT], qk[:, START[t]:START[t] + P], sel[:],
                              start=True, stop=True)
                return last

            def broadcast(b, j):
                if j == 0:
                    pe.wait_ge(s_at, b + 1)
                if b == B - 1 and j >= 1:
                    pe.wait_ge(s_ue, unit_no[("bc", b, j)] - 1)
                else:
                    fill(("bc", b, j))
                for t in range(NT):
                    for a in range(2):
                        for hd in range(2):
                            i = hd * NT + t
                            last = mm(bc_banks(b, j)[hd * D:(hd + 1) * D, t * P:(t + 1) * P],
                                      ath[:, a, j, i:i + 1].to_broadcast([P, D]), idh[:],
                                      start=(a == 0), stop=(a == 1))
                last.then_inc(s_uf, 1)

            def out_proj(b, n):
                if b == 0 and n == 0:
                    pe.wait_ge(s_w0, 32)
                pe.wait_ge(s_av, NPAIR * (b + 1))
                fill(("o", b, n))
                for t in range(3 * n, 3 * n + 3):
                    for j in range(NPAIR):
                        last = mm(U[:, t * D:(t + 1) * D], avT[:, j, t * P:(t + 1) * P], w0p[:, j, :],
                                  start=(j == 0), stop=(j == NPAIR - 1))
                last.then_inc(s_uf, 1)

            def x2_T(b):
                pe.wait_ge(s_xh2, b + 1)
                fill(("t", b, 0))
                for t in range(NT):
                    last = nc.tensor.transpose(U[0:D + 1, t * P:(t + 1) * P], xrow[:, b * NT + t, 0:D + 1], idf[:])
                last.then_inc(s_uf, 1)

            def logits(b, n):
                fill(("l", b, n))
                if n == 0:
                    pe.wait_ge(s_w1c, 1)
                    pe.wait_ge(s_b1, 16)
                for t in range(3):
                    last = mm(U[:, t * 256:(t + 1) * 256], xT2[:, (3 * n + t) * P:(3 * n + t + 1) * P], w1T[:],
                              start=True, stop=True)
                last.then_inc(s_uf, 1)

            def ranks(b):
                pe.wait_ge(s_m7, b + 1)
                fill(("r", b, 0))
                for t in range(NT):
                    mm(U[:, t * P:(t + 1) * P], tri[:], m7[:, b * NT + t, :], start=True, stop=False)
                    last = mm(U[:, t * P:(t + 1) * P], ones[:], run[:, t, :], start=False, stop=True)
                last.then_inc(s_uf, 1)

            def extra(u, n):
                es = extras(u)
                if n >= len(es) or es[n] is None:
                    return
                kind, b, k = es[n]
                if kind == "bc":
                    broadcast(b, k)
                elif kind == "o":
                    out_proj(b, k)
                elif kind == "t":
                    x2_T(b)
                elif kind == "l":
                    logits(b, k)
                else:
                    ranks(b)

            def scores(u, i):
                hd, t = divmod(i, NT)
                n = 2 * NT * u + i
                if i == 0:
                    pe.wait_ge(s_st[u % 3], 16 * 8 * (u // 3 + 1))
                if n >= 3:
                    pe.wait_ge(s_exp, n - 2)
                for a in range(2):
                    for c0, c1 in ((0, 512), (512, N)):
                        last = mm(S[n % 3][:, c0:c1], kst[:, u % 3, a, hd, START[t]:START[t] + P],
                                  qst[:, u % 3, hd, c0:c1], start=(a == 0), stop=(a == 1))
                last.then_inc(s_score, 1)

            pe.wait_ge(s_xhT, B)
            pe.wait_ge(s_wq, 1)
            pe.wait_ge(s_id, 2)
            pe.wait_ge(s_w1c, 1)
            for w in range(AHEAD):
                for kind in "qkv":
                    project(kind, w)
            for u in range(NU + NPAIR):
                for i in range(2 * NT):
                    if u < NU:
                        scores(u, i)
                    if i in (1, 3, 5) and u + AHEAD < NU:
                        project("qkv"[i // 2], u + AHEAD)
                    if i == 5 and u + AHEAD == NU:
                        fill(("d", NU - 1, 0))
                        diagonal(NU - 1, range(NT)).then_inc(s_uf, 1)
                    if i in (7, 9, 11):
                        extra(u, (i - 7) // 2)
            pe.wait_ge(s_m7, B)
            pe.wait_ge(s_ue, len(units))
            mm(U[:, 0:1], run[:, NT, :], ones[:, 0:1], start=True, stop=True).then_inc(s_cnt, 1)
            pe.wait_ge(s_og, 1)
            mm(U[:, 128:256], og[:].to_broadcast([P, P]), tri[:], start=True, stop=True)
            mm(U[:, 256:257], tri_i[:], og[:], start=True, stop=True).then_inc(s_pre, 1)
            pe.wait_ge(s_ind, 1)
            mm(U[0:32, 512:512 + OVG], ones[:, 0:32], ind[:], start=True, stop=True).then_inc(s_lam, 1)

            tv = wlow.rearrange("p (e o) -> p e o", o=D)
            pe.wait_ge(s_tab, 16 * 2)
            pe.wait_ge(s_low, 16 * 2 * sum(2 ** (lvs[-1] - lv) for _, lvs in LOW for lv in lvs))
            pe.wait_ge(s_zl, 2)

            def xs_T(m):
                pe.wait_ge(s_xsr[m % NX], 16 * (m // NX + 1))
                if m >= 2:
                    pe.wait_ge(s_xc, m - 1)
                for t in range(4):
                    last = nc.tensor.transpose(S[0][0:D + 1, 512 * (m % 2) + t * P:512 * (m % 2) + (t + 1) * P],
                                               xs[:, m % NX, t, 0:D + 1], idf[:])
                last.then_inc(s_xp, 1)

            def tile_ready(k):
                if k % 4 == 0:
                    pe.wait_ge(s_xc, k // 4 + 1)

            def bank_ready(n):
                if n >= ST_TILES + NY:
                    pe.wait_ge(s_yv, n - NY - ST_TILES + 1)
                elif n >= NY:
                    pe.wait_ge(s_wy, n - NY + 1)

            def tile_products(k):
                tile_ready(k)
                bank_ready(k)
                y = y_bank(k).rearrange("p (l o) -> p l o", o=D)
                xk = xsT[:, k // 4 % 3, (k % 4) * P:(k % 4 + 1) * P]
                mm(y[:, 0:4, :], xk, tv[:, T03 + 4 * (k // 4):T03 + 4 * (k // 4) + 4, :], start=True, stop=True)
                mm(y[:, 4:6, :], xk, tv[:, T45 + 2 * k:T45 + 2 * k + 2, :], start=True, stop=True)
                for g in range(2):
                    gs = slice(2 * G * g, 2 * G * (g + 1))
                    mm(y[gs, 6, :], xk[:, gs], tv[:, T6 + 2 * k + g, :], start=True, stop=True)
                for g in range(4):
                    gs = slice(G * g, G * (g + 1))
                    last = mm(y[gs, 7, :], xk[:, gs], w7[:, (4 * k + g) * D:(4 * k + g + 1) * D],
                              start=True, stop=True)
                last.then_inc(s_y, 1)

            def load_leaves(k):
                kk = k - ST_TILES
                return [nc.tensor.value_load(lami[0:1, 2 * kk + i:2 * kk + i + 1], min_val=0,
                                             max_val=LEAVES * LEAVES - 1) for i in range(2)]

            def overflow_products(k, pairs):
                following = None

                def node(g, sh):
                    if g % 2:
                        return pairs[g // 2] >> (7 + sh)
                    return (pairs[g // 2] >> sh) & (LEAVES - 1 >> sh)

                tile_ready(k)
                xk = xsT[:, k // 4 % 3, (k % 4) * P:(k % 4 + 1) * P]
                for g in range(4):
                    if g == 2 and k % 4 < 3:
                        following = load_leaves(k + 1)
                    bank_ready(banks(k) + g)
                    y = y_bank(banks(k) + g)[0:G, :]
                    xg = xk[:, G * g:G * (g + 1)]
                    mm(y[:, 0:4 * D], xg, wlow[:, bass.ds(node(g, 4) * (4 * D) + T03 * D, 4 * D)],
                       start=True, stop=True)
                    mm(y[:, 4 * D:6 * D], xg, wlow[:, bass.ds(node(g, 2) * (2 * D) + T45 * D, 2 * D)],
                       start=True, stop=True)
                    mm(y[:, 6 * D:7 * D], xg, wlow[:, bass.ds(node(g, 1) * D + T6 * D, D)],
                       start=True, stop=True)
                    mm(y[:, 7 * D:8 * D], xg, w7all[:, bass.ds(node(g, 0) * D, D)],
                       start=True, stop=True).then_inc(s_y, 1)
                return following

            pe.wait_ge(s_goff, 1)
            xs_T(0)
            for k in range(ST_TILES):
                if k % 4 == 0 and k + 4 < ST_TILES:
                    xs_T(k // 4 + 1)
                tile_products(k)
            groups = pe.value_load(nact[0:1, 0:1], min_val=0, max_val=OVG)
            for m in range(ST_TILES // 4, F_TILES // 4):
                with pe.If(groups > 4 * (4 * m - ST_TILES)):
                    xs_T(m)
                    pairs = load_leaves(4 * m)
                    for k in range(4 * m, 4 * m + 4):
                        pairs = overflow_products(k, pairs)

        @block.scalar
        def _(act):
            sc_ = nc.scalar
            def x_copy(b):
                act.wait_ge(s_xtp, b + 1)
                if b >= 2:
                    act.wait_ge(s_cv, b - 1)
                xp = S[0][:, 512 * (b % 2):512 * (b % 2) + 384].bitcast(bf16).rearrange("p (j n) -> p j n", j=XB)
                sc_.copy(xT[:, b % 2, :].rearrange("p (j n) -> p j n", j=XB), xp[:, :, 0:XP]).then_inc(s_xtc, 1)

            x_copy(0)
            x_copy(1)
            act.wait_ge(s_bnb, 1)
            sc_.copy(bn[:].rearrange("p a d -> p (a d)"), U[:, 512:512 + 2 * D]).then_inc(s_bn, 1)
            for b in range(B):
                if b + 2 < B:
                    x_copy(b + 2)
                act.wait_ge(s_xn, b + 1)
                if b >= 1:
                    act.wait_ge(s_xhp, b)
                sc_.copy(xhl[:, :, 0, :], xn[:]).then_inc(s_hi, 1)
                act.wait_ge(s_xhp, b + 1)
                xp = S[2][:, 512 * (b % 2):512 * (b % 2) + 384].bitcast(f16)
                sc_.copy(xhT[:, b * N:b * N + START[-1]], xp[:, 0:START[-1]])
                sc_.copy(xhT[:, b * N + START[-1]:(b + 1) * N], xp[:, (NT - 1) * P:]).then_inc(s_xhT, 1)
            act.wait_ge(s_w1p, 1)
            sc_.copy(w1T[0:D, 0:NODES], U[0:D, 0:NODES])
            sc_.mul(w1T[0:D, NODES:256], idf[0:D, 0:1], 0.0).then_inc(s_w1c, 1)

            def diag_copy(w):
                b, j = divmod(w, NPAIR)
                if b >= 2 and j == 0:
                    act.wait_ge(s_ex1, b - 1)
                return sc_.copy(dg[:, b % 2, j, :], U[:, U_D:U_D + 2 * NT])

            def qkv_out(kind, w):
                b, j = divmod(w, NPAIR)
                if w == 0:
                    act.wait_ge(s_bq8, 1)
                act.wait_ge(s_uf, unit_no[(kind, w, 0)] + 1)
                if kind != "v" and w >= 2:
                    act.wait_ge(s_prod, w - 1)
                if kind == "v" and w >= 8:
                    act.wait_ge(s_av, w - 7)
                dst = {"q": q32[:, w % 2, 0:QN], "k": k32[:, w % 2, 0:QN], "v": vT[:, w % 8, 0:QN]}[kind]
                base = "qkv".index(kind) * T + b * N
                for s in range(3):
                    g = (base + s) % 3
                    bv = (bq8 if kind == "q" else bq)[:, g * NPAIR + j:g * NPAIR + j + 1]
                    last = sc_.activation(dst.rearrange("p (n s) -> p n s", s=3)[:, :, s],
                                          U[:, 256 * s:256 * s + NP3], ACT.Identity, bias=bv,
                                          scale=D ** -0.5 if kind == "q" else 1.0)
                if kind == "v" and w >= 1:
                    last = diag_copy(w - 1)
                last.then_inc(s_ue, 1)

            def exps(u, i):
                n = 2 * NT * u + i
                b, j = divmod(u, NPAIR)
                act.wait_ge(s_max, n + 1)
                if i == 0 and j == 0 and b >= 2:
                    act.wait_ge(s_at, b - 1)
                sc_.activation(S[n % 3][:, 0:N], S[n % 3][:, 0:N], ACT.Exp, bias=nm[:, b % 2, j, i:i + 1],
                               accum_out=sm[:, b % 2, j, i:i + 1]).then_inc(s_exp, 1)

            def diag_exp(b):
                act.wait_ge(s_ex1, b + 1)
                sc_.activation(at[:, b % 2], at[:, b % 2], ACT.Exp).then_inc(s_ex2, 1)

            def extra(u, n):
                es = extras(u)
                if n >= len(es) or es[n] is None:
                    return
                kind, b, k = es[n]
                if kind == "t":
                    act.wait_ge(s_uf, unit_no[("t", b, 0)] + 1)
                    sc_.copy(xT2[:], U[0:D + 1, 0:NT * P]).then_inc(s_ue, 1)
                elif kind == "l":
                    act.wait_ge(s_uf, unit_no[("l", b, k)] + 1)
                    if b >= 1 and k == 0:
                        act.wait_ge(s_m7, b)
                    sc_.copy(L[:, 3 * k:3 * k + 3, :].rearrange("p t n -> p (t n)"),
                             U[:, 0:768]).then_inc(s_ue, 1)

            for w in range(AHEAD):
                for kind in "qkv":
                    qkv_out(kind, w)
            for u in range(NU + NPAIR):
                for i in range(2 * NT):
                    if u < NU:
                        exps(u, i)
                    if i in (0, 2, 4) and u + AHEAD < NU:
                        qkv_out("qkv"[i // 2], u + AHEAD)
                    if i == 4 and u + AHEAD == NU:
                        act.wait_ge(s_uf, unit_no[("d", NU - 1, 0)] + 1)
                        diag_copy(NU - 1).then_inc(s_ue, 1)
                    if i == 1 and u % NPAIR == 0 and u >= NPAIR:
                        diag_exp(u // NPAIR - 1)
                    if i in (6, 8, 10):
                        extra(u, (i - 6) // 2)
            act.wait_ge(s_zl, 2)
            sc_.activation(warm[:], half[0:1, 0:1], ACT.Gelu)

            def path_weights(m):
                act.wait_ge(s_xsr[m % NX], 16 * (m // NX + 1))
                w = xs[:, m % NX, :, C_W:C_H]
                sc_.activation(w, w, ACT.Gelu).then_inc(s_gelu, 1)

            def xs_copy(m):
                act.wait_ge(s_xp, m + 1)
                if m >= 3:
                    act.wait_ge(s_y, banks(4 * (m - 2)))
                sc_.copy(xsT[0:D + 1, m % 3, :], S[0][0:D + 1, 512 * (m % 2):512 * (m % 2) + 512]).then_inc(s_xc, 1)

            for m in range(ST_TILES // 4):
                path_weights(m)
                xs_copy(m)
            act.wait_ge(s_goff, 1)
            groups = act.value_load(nact[0:1, 0:1], min_val=0, max_val=OVG)
            for m in range(ST_TILES // 4, F_TILES // 4):
                with act.If(groups > 4 * (4 * m - ST_TILES)):
                    path_weights(m)
                    xs_copy(m)
                    for k in range(4 * m, 4 * m + 4):
                        if k >= ST_TILES + 2:
                            act.wait_ge(s_wy, k - 1)
                        for g in range(4):
                            act.wait_ge(s_y, banks(k) + g + 1)
                            sc_.copy(yv[g * G:(g + 1) * G, k % 2, :],
                                     y_bank(banks(k) + g)[0:G, :]).then_inc(s_yv, 1)

        @block.vector
        def _(dve):
            v = nc.vector
            link = chain(dve, vs)

            def signs(b):
                dve.wait_ge(s_xin[b], 16)
                v.tensor_scalar(sgn[:, b * XB:(b + 1) * XB, :], xin[:, b * XB:(b + 1) * XB, :], 0.0, 0.5,
                                ALU.is_ge, ALU.subtract).then_inc(s_sgn, 1)

            signs(0)
            dve.wait_ge(s_par, 16 * 5)
            v.tensor_scalar(kq[:], kk[:], 0.0, 0.5, ALU.is_ge, ALU.subtract).then_inc(s_kq, 1)
            for b in range(1, B):
                signs(b)

            dve.wait_ge(s_w, 32)
            for g in range(3):
                gs = slice(g * H * D, (g + 1) * H * D)
                src = wst[:, gs].rearrange("p (d h) -> p h d", h=H)
                hi = wq[:, 0, gs].rearrange("p (h d) -> p h d", h=H)
                lo = wq[:, 1, gs].rearrange("p (h d) -> p h d", h=H)
                link(v.tensor_copy(hi, src))
                last = v.tensor_tensor(lo, src, hi, ALU.subtract)
            last.then_inc(s_wq, 1)

            def center(b):
                dve.wait_ge(s_cv, b + 1)
                hv = xrow[:, b * NT:(b + 1) * NT, C_H:C_ID]
                cv = S[1][:, 512 * (b % 2):512 * (b % 2) + NT * D].rearrange("p (t d) -> p t d", t=NT)
                if b == 0:
                    dve.wait_ge(s_bn, 1)
                c, l = cent[:, b % 2], ln1[:, b % 2]
                v.tensor_tensor(hv, cv, bn[:, 0:1, :].to_broadcast([P, NT, D]), ALU.mult).then_inc(s_h, 1)
                dve.wait_ge(s_h, b + 1)
                link(v.tensor_tensor(hv, hv, bn[:, 1:2, :].to_broadcast([P, NT, D]), ALU.add))
                link(v.tensor_reduce(l[:, 0, :], hv, X, ALU.add))
                link(v.tensor_scalar(l[:, 0, :], l[:, 0, :], -1.0 / D, None, ALU.mult))
                link(v.tensor_tensor(c, hv, l[:, 0, :].unsqueeze(2).to_broadcast([P, NT, D]), ALU.add))
                link(v.tensor_tensor(sq[:], c, c, ALU.mult))
                v.tensor_reduce(l[:, 1, :], sq[:], X, ALU.add).then_inc(s_sum, 1)

            def normalise(b):
                dve.wait_ge(s_rs, b + 1)
                if b >= 1:
                    dve.wait_ge(s_xhl, b)
                v.tensor_tensor(xn[:], cent[:, b % 2], ln1[:, b % 2, 3, :].unsqueeze(2).to_broadcast([P, NT, D]),
                                ALU.mult).then_inc(s_xn, 1)

            center(0)
            for b in range(B):
                if b + 1 < B:
                    center(b + 1)
                normalise(b)
            dve.wait_ge(s_bq, 32)
            for a in range(2):
                hs = slice(a * D, (a + 1) * D)
                ins = v.tensor_copy(bq[hs, :].rearrange("p (g j) -> p g j", g=3), bqn[hs, :, a::2])
            link(ins)
            v.tensor_scalar(bq8[:], bq[:], D ** -0.5, None, ALU.mult).then_inc(s_bq8, 1)

            def hi_cast(kind, w):
                n = "qk".index(kind)
                dve.wait_ge(s_ue, unit_no[(kind, w, 0)] + 1)
                if w >= 2:
                    dve.wait_ge(s_st[(w - 2) % 3], 16 * 8 * ((w - 2) // 3 + 1))
                v.tensor_copy(hl[:, w % 2, n, 0, 0:QN], (q32, k32)[n][:, w % 2, 0:QN]).then_inc((s_qc, s_kc)[n], 1)

            def maxima(u, i):
                n = 2 * NT * u + i
                b, j = divmod(u, NPAIR)
                dve.wait_ge(s_score, n + 1)
                v.tensor_reduce(nm[:, b % 2, j, i:i + 1], S[n % 3][:, 0:N], X, ALU.max, negate=True).then_inc(s_max, 1)

            def diag_weights(b):
                dve.wait_ge(s_exp, 2 * NT * NPAIR * (b + 1))
                dve.wait_ge(s_ue, diag_unit(NPAIR * b + NPAIR - 1) + 1)
                v.reciprocal(sm[:, b % 2], sm[:, b % 2])
                v.tensor_tensor(at[:, b % 2], dg[:, b % 2], nm[:, b % 2], ALU.add).then_inc(s_ex1, 1)

            def diag_scale(b):
                dve.wait_ge(s_ex2, b + 1)
                link(v.tensor_tensor(at[:, b % 2], at[:, b % 2], sm[:, b % 2], ALU.mult))
                if b >= 1:
                    dve.wait_ge(s_uf, unit_no[("bc", b - 1, NPAIR - 1)] + 1)
                link(v.tensor_copy(ath[:, 0], at[:, b % 2]))
                v.tensor_tensor(ath[:, 1], at[:, b % 2], ath[:, 0], ALU.subtract).then_inc(s_at, 1)

            def extra(u, n):
                es = extras(u)
                if n >= len(es) or es[n] is None:
                    return
                kind, b, k = es[n]
                bt = slice(b * NT, (b + 1) * NT)
                if kind == "bc":
                    dve.wait_ge(s_uf, unit_no[("bc", b, k)] + 1)
                    if b >= 1 and k == 0:
                        dve.wait_ge(s_uf, unit_no[("o", b - 1, 1)] + 1)
                    c = START[-1]
                    e = (NT - 1) * P
                    vt = vT[:, (NPAIR * b + k) % 8, :]
                    bc = bc_banks(b, k)
                    v.tensor_tensor(avT[:, k, 0:e], vt[:, 0:e], bc[:, 0:e], ALU.mult)
                    v.tensor_tensor(avT[:, k, e:], vt[:, c:N], bc[:, e:NT * P], ALU.mult).then_inc(s_av, 1)
                    dve.wait_ge(s_av, NPAIR * b + k + 1)
                    dve.sem_inc(s_ue, 1)
                elif kind == "o":
                    dve.wait_ge(s_uf, unit_no[("o", b, k)] + 1)
                    if k == 0:
                        dve.wait_ge(s_hb, b + 1)
                    ho = xrow[:, b * NT + 3 * k:b * NT + 3 * k + 3, C_H:C_ID]
                    v.tensor_tensor(ho, U[:, 3 * k * D:(3 * k + 3) * D].rearrange("p (t d) -> p t d", t=3), ho,
                                    ALU.add).then_inc(s_ue, 1)
                    if k == 1:
                        dve.wait_ge(s_ue, unit_no[("o", b, 1)] + 1)
                        v.tensor_reduce(ln2[:, 0, :], xrow[:, bt, C_H:C_ID], X, ALU.add).then_inc(s_h2, 1)
                elif kind == "r":
                    dve.wait_ge(s_uf, unit_no[("r", b, 0)] + 1)
                    rm = gt[:]
                    v.tensor_tensor(rm, U[:, 0:NT * P].rearrange("p (t n) -> p t n", t=NT), m7[:, bt, :],
                                    ALU.mult).then_inc(s_ue, 1)
                    dve.wait_ge(s_ue, unit_no[("r", b, 0)] + 1)
                    v.tensor_reduce(rank[:, bt], rm, X, ALU.add).then_inc(s_rk, 1)
                    if b < B - 1:
                        path_logits(b)
                    dve.wait_ge(s_rk, b + 1)
                    static_slots(b)

            def ln2_sumsq(b):
                dve.wait_ge(s_c2, b + 1)
                v.tensor_reduce(ln2[:, 1, :], sq[:], X, ALU.add).then_inc(s_ss2, 1)

            def ln2_last():
                bt = slice((B - 1) * NT, TT)
                dve.wait_ge(s_h2, B)
                link(v.tensor_scalar(ln2[:, 2, :], ln2[:, 0, :], -1.0 / D, None, ALU.mult))
                link(v.tensor_tensor(cent[:, 0], xrow[:, bt, C_H:C_ID],
                                     ln2[:, 2, :].unsqueeze(2).to_broadcast([P, NT, D]), ALU.add))
                link(v.tensor_tensor(sq[:], cent[:, 0], cent[:, 0], ALU.mult))
                v.tensor_reduce(ln2[:, 1, :], sq[:], X, ALU.add).then_inc(s_ss2, 1)
                dve.wait_ge(s_rs2, 1)
                v.tensor_tensor(xrow[:, bt, 0:D], cent[:, 0],
                                ln2[:, 3, :].unsqueeze(2).to_broadcast([P, NT, D]), ALU.mult).then_inc(s_xh2, 1)

            def static_slots(b):
                bt = slice(b * NT, (b + 1) * NT)
                link(v.tensor_scalar(lgb[:], lg[:, bt, 0:DEPTH - 1], 0.0, None, ALU.is_gt))
                v.scalar_tensor_tensor(xrow[:, bt, C_W:C_H], lg[:, bt], -1.0, lg[:, bt], ALU.mult, ALU.max)
                link(v.tensor_tensor(lgb[:], lgb[:], pw2[:].unsqueeze(1).to_broadcast([P, NT, DEPTH - 1]), ALU.mult))
                link(v.tensor_reduce(leaf[:, bt], lgb[:], X, ALU.add))
                link(v.tensor_scalar(sc[:, 0, bt], rank[:, bt], float(G), float(BIG), ALU.is_ge, ALU.mult))
                link(v.tensor_tensor(sc[:, 1, bt], leaf[:, bt], rank[:, bt], ALU.add))
                link(v.tensor_tensor(sc[:, 0, bt], sc[:, 0, bt], sc[:, 1, bt], ALU.add))
                last = slice(TT - 1 - (B - 1 - b) * NT, TT - (B - 1 - b) * NT)
                link(v.tensor_tensor(sc[:, 0, last], sc[:, 0, last], dup_out[:], ALU.add))
                v.tensor_copy(slot[:, bt], sc[:, 0, bt]).then_inc(s_slot, 1)

            def path_logits(b):
                dve.wait_ge(s_ml, b + 1)
                for lv in range(DEPTH):
                    n = 2 ** lv
                    last = v.tensor_reduce(lg[:, b * NT:(b + 1) * NT, lv], ML[:, :, n - 1:2 * n - 1], X, ALU.add)
                last.then_inc(s_lg, 1)
                dve.wait_ge(s_lg, b + 1)

            for w in range(AHEAD):
                hi_cast("q", w)
                hi_cast("k", w)
            for u in range(NU + NPAIR):
                b, ph = u // NPAIR - 1, u % NPAIR
                for i in range(2 * NT):
                    if u < NU:
                        maxima(u, i)
                    if b >= 0 and ph == 0 and i == 1:
                        diag_weights(b)
                    if b >= 0 and ph == 0 and i == 3:
                        diag_scale(b)
                    if i in (3, 5) and u + AHEAD < NU:
                        hi_cast("qk"[(i - 3) // 2], u + AHEAD)
                    if i in (7, 9, 11):
                        if b == B - 1 and ph == 3 and i == 11:
                            path_masks(b, dve, v, link)
                            leaf_masks(b, dve, v, link)
                            path_logits(b)
                        extra(u, (i - 6) // 2)
                    if 0 <= b < B - 1 and ph == 2 and i == 2:
                        ln2_sumsq(b)
                    if b == B - 1 and ph == 2 and i == 2:
                        ln2_last()

            dve.wait_ge(s_cnt, 1)
            link(v.tensor_scalar(ogi[:, 0:1], U[:, 0:1], -1.0, float(G - 1), ALU.add, ALU.max))
            link(v.tensor_scalar(ogi[:, 1:2], ogi[:, 0:1], 5, None, ALU.arith_shift_right))
            v.tensor_copy(og[:], ogi[:, 1:2]).then_inc(s_og, 1)
            dve.wait_ge(s_pre, 1)
            v.tensor_copy(ovb[:], U[:, 128:256])
            link(v.tensor_copy(endg[:, 0:1], U[:, 256:257]))
            v.tensor_scalar(ind[:], giota[:], endg[:, 0:1], None, ALU.is_ge).then_inc(s_ind, 1)
            om = lm[:].rearrange("p a t n -> p (a t n)")[:, 0:TT * LEAVES // 2].bitcast(bf16).rearrange(
                "p (t n) -> p t n", t=TT)
            link(v.tensor_tensor(om, m7[:], ovb[:].unsqueeze(1).to_broadcast([P, TT, LEAVES]), ALU.mult))
            n = LEAVES // 2
            while n >= 16:
                link(v.tensor_tensor(om[:, :, 0:n], om[:, :, 0:n], om[:, :, n:2 * n], ALU.add))
                n //= 2
            link(v.tensor_reduce(sc[:, 0, :], om[:, :, 0:2 * n], X, ALU.add))
            link(v.tensor_scalar(sc[:, 0, :], sc[:, 0, :], float(G), float(STAT - G), ALU.mult, ALU.add))
            link(v.tensor_scalar(sc[:, 1, :], rank[:], float(G), float(BIG), ALU.is_lt, ALU.mult))
            link(v.tensor_tensor(sc[:, 1, :], sc[:, 1, :], rank[:], ALU.add))
            link(v.tensor_tensor(sc[:, 2, :], sc[:, 0, :], sc[:, 1, :], ALU.add))
            v.tensor_copy(oslot[:], sc[:, 2, :]).then_inc(s_oslot, 1)
            dve.wait_ge(s_lam, 1)
            link(v.tensor_scalar(act_f[:, 0:OVG], U[0:1, 512:512 + OVG], float(LEAVES), None, ALU.is_lt))
            link(v.tensor_reduce(act_f[:, OVG:OVG + 1], act_f[:, 0:OVG], X, ALU.add))
            link(v.tensor_copy(nact[:], act_f[:, OVG:OVG + 1]))
            link(v.tensor_scalar(lamf[:], U[0:1, 512:512 + OVG], float(LEAVES - 1), None, ALU.min))
            v.scalar_tensor_tensor(lami[:], lamf[:, 1::2], float(LEAVES), lamf[:, 0::2], ALU.mult,
                                   ALU.add).then_inc(s_goff, 1)

            def weigh(k):
                if k % 4 == 0:
                    dve.wait_ge(s_gelu, k // 4 + 1)
                wk = xs[:, (k // 4) % NX, k % 4, C_W:C_H]
                if k < ST_TILES:
                    y = y_bank(k)
                    dve.wait_ge(s_y, k + 1)
                else:
                    y = yv[:, k % 2, :]
                    dve.wait_ge(s_yv, 4 * (k - ST_TILES + 1))
                v.tensor_tensor(wy[:, k % 2].rearrange("p (l o) -> p l o", o=D), y.rearrange("p (l o) -> p l o", o=D),
                                wk.unsqueeze(2).to_broadcast([P, DEPTH, D]), ALU.mult).then_inc(s_wy, 1)

            def sum_levels(k):
                if k >= NO:
                    dve.wait_ge(s_outr[k % NO], 16 * (k // NO))
                dve.wait_ge(s_wy, k + 1)
                v.tensor_reduce(yo[:, k % NO, :], wy[:, k % 2].rearrange("p (l o) -> p o l", o=D), X,
                                ALU.add).then_inc(s_sl, 1)

            def add_residual(k):
                dve.wait_ge(s_sl, k + 1)
                o = yo[:, k % NO, :]
                v.tensor_tensor(o, o, xs[:, (k // 4) % NX, k % 4, C_H:C_ID], ALU.add).then_inc(s_yo, 1)

            for k in range(ST_TILES):
                weigh(k)
                if k >= 1:
                    add_residual(k - 1)
                sum_levels(k)
            add_residual(ST_TILES - 1)
            dve.wait_ge(s_goff, 1)
            groups = dve.value_load(nact[0:1, 0:1], min_val=0, max_val=OVG)
            for m in range(ST_TILES // 4, F_TILES // 4):
                with dve.If(groups > 4 * (4 * m - ST_TILES)):
                    for k in range(4 * m, 4 * m + 4):
                        weigh(k)
                        sum_levels(k)
                        add_residual(k)


_INS = ["x", "L0_tok_kernel", "L0_tok_bias", "L0_tok_beta", "L0_tok_moving_mean", "L0_tok_moving_var",
        "L0_attn_Wqkv", "L0_attn_bqkv", "L0_attn_W0", "L0_attn_b0", "L0_ffn_w1s", "L0_ffn_b1s",
        "L0_ffn_w2s", "L0_ffn_b2s"]


def kernel(**inputs):
    import concourse.bacc as _bacc
    from concourse import mybir as _mybir
    from concourse.bass_utils import run_bass_kernel_spmd as _run

    nc = _bacc.Bacc("TRN2", target_bir_lowering=False, num_devices=1)
    arrays, args = {}, []
    for name in _INS:
        a = np.ascontiguousarray(inputs[name])
        arrays[f"in_{name}"] = a
        args.append(nc.dram_tensor(f"in_{name}", a.shape, _mybir.dt.from_np(a.dtype), kind="ExternalInput").ap())
    rows = nc.dram_tensor("sorted_rows", (SLOTS, RW), _mybir.dt.float32).ap()
    out = nc.dram_tensor("out_0", (B, N, D), _mybir.dt.float32, kind="ExternalOutput").ap()
    tower(nc, *args, rows, out)
    r = _run(nc, [arrays], core_ids=[0])
    return r.results[0]["out_0"]
```
